# Optimizing a Trainium2 kernel written in Bass

```python
import numpy as np
import jax
import jax.numpy as jnp

def _softmax(x, axis=-1):
    return jax.nn.softmax(x, axis=axis)

def _gelu(x):
    return jax.nn.gelu(x, approximate=True)

def _silu(x):
    return jax.nn.silu(x)

def _sigmoid(x):
    return jax.nn.sigmoid(x)

def _layernorm(x, axis=-1, eps=1e-05):
    m = jnp.mean(x, axis=axis, keepdims=True)
    v = jnp.var(x, axis=axis, keepdims=True)
    return (x - m) / jnp.sqrt(v + eps)

def _scatter_add(tgt, idx, src, axis=0):
    return tgt.at[idx].add(src)

def _segment_sum(src, seg, n):
    return jax.ops.segment_sum(src, seg, n)
kernel_name = 'mk_adj_resnorm_d2_adj_r2_3a7ebd'

def setup_inputs(seed: int=0):
    np.random.seed(seed)
    _w = jnp.asarray

    def _rec_inputs():
        import jax
        import jax.numpy as jnp
        _gk = jax.random.key(seed)
        x = 7.22e-05 + 1 * jax.random.normal(jax.random.fold_in(_gk, 1), (16, 512, 128), jnp.float32)
        _a = jax.random.bernoulli(jax.random.fold_in(_gk, 2), 0.03125, (512, 512))
        _a = jnp.logical_or(_a, jnp.swapaxes(_a, -1, -2))
        _a = jnp.logical_or(_a, jnp.eye(512, dtype=bool))
        _af = _a.astype(jnp.float32)
        _af = _af * jax.random.uniform(jax.random.fold_in(_gk, 3), (512, 512), jnp.float32, 0.05, 0.000976562)
        adj = _af
        return (x, adj)
    x, adj = _rec_inputs()

    def _L0_gnn_setup():
        import jax, jax.numpy as jnp
        import numpy as np
        N_STEPS = 8
        SPATIAL_SCALE = 1.0
        key = jax.random.key(seed)
        ks = jax.random.split(key, 6)
        B, N, D = (32, 512, 128)
        x = jax.random.normal(ks[0], (B, N, D), dtype=jnp.float32)
        adj_mx = jax.random.uniform(ks[1], (N, N), dtype=jnp.float32) / N
        alpha_train = jnp.ones((N,), dtype=jnp.float32)
        w = jnp.eye(D, dtype=jnp.float32) + 0.01 * jax.random.normal(ks[2], (D, D), dtype=jnp.float32)
        d = jax.random.uniform(ks[3], (D,), dtype=jnp.float32)
        fc_in_w = jax.random.normal(ks[4], (D, D), dtype=jnp.float32) * (1.0 / np.sqrt(D))
        fc_in_b = jnp.zeros((D,), dtype=jnp.float32)
        return {'x': x, 'adj_mx': adj_mx, 'alpha_train': alpha_train, 'w': w, 'd': d, 'fc_in_w': fc_in_w, 'fc_in_b': fc_in_b, 'vt': 0}
    _L0_gnn_all = _L0_gnn_setup()
    _L0_gnn_in = {k: v for k, v in _L0_gnn_all.items() if k in ('alpha_train', 'w', 'd', 'fc_in_w', 'fc_in_b')}
    del _L0_gnn_all

    def _L1_gnn_setup():
        import jax, jax.numpy as jnp
        import numpy as np
        B, N, IN_DIM, OUT_DIM, H = (2, 2048, 128, 128, 4)
        HEAD_DIM = OUT_DIM // H
        EDGE_P = 0.01
        key = jax.random.key(seed)
        k1, k2, k3 = jax.random.split(key, 3)
        h = jax.random.normal(k1, (B, N, IN_DIM), dtype=jnp.float32)
        W = jax.random.normal(k2, (IN_DIM, 3 * OUT_DIM), dtype=jnp.float32) / np.sqrt(IN_DIM)
        adj = (jax.random.uniform(k3, (N, N)) < EDGE_P).astype(jnp.float32)
        adj = jnp.maximum(adj, jnp.eye(N, dtype=jnp.float32))
        return {'h': h, 'W': W, 'adj': adj}
    _L1_gnn_all = _L1_gnn_setup()
    _L1_gnn_in = {k: v for k, v in _L1_gnn_all.items() if k in ('W',)}
    del _L1_gnn_all
    return {'x': x, 'adj': adj, 'L0_gnn_alpha_train': _L0_gnn_in['alpha_train'], 'L0_gnn_w': _L0_gnn_in['w'], 'L0_gnn_d': _L0_gnn_in['d'], 'L0_gnn_fc_in_w': _L0_gnn_in['fc_in_w'], 'L0_gnn_fc_in_b': _L0_gnn_in['fc_in_b'], 'L1_gnn_W': _L1_gnn_in['W']}

def reference(x, adj, L0_gnn_alpha_train, L0_gnn_w, L0_gnn_d, L0_gnn_fc_in_w, L0_gnn_fc_in_b, L1_gnn_W):
    import jax
    import jax.numpy as jnp

    def _L0_gnn_ref(x, adj_mx, alpha_train, w, d, fc_in_w, fc_in_b, vt):
        import jax, jax.numpy as jnp
        import numpy as np
        N_STEPS = 8
        SPATIAL_SCALE = 1.0
        x0 = jax.lax.stop_gradient(x)
        h = jnp.einsum('bnd,ed->bne', x, fc_in_w) + fc_in_b
        alph = jax.nn.sigmoid(alpha_train)[:, None]
        d_clamped = jnp.clip(d, 0.0, 1.0)
        w_eff = w * d_clamped @ w.T
        dt = jnp.float32(SPATIAL_SCALE / N_STEPS)

        def euler_step(h, _):
            ax = jnp.einsum('nm,bmd->bnd', adj_mx, h)
            f = alph * 0.5 * (ax - h) + h @ w_eff - h + x0
            return (h + dt * f, None)
        h, _ = jax.lax.scan(euler_step, h, None, length=N_STEPS)
        return h

    def _L1_gnn_ref(h, W, adj):
        import jax, jax.numpy as jnp
        import numpy as np
        B, N, IN_DIM, OUT_DIM, H = (2, 2048, 128, 128, 4)
        HEAD_DIM = OUT_DIM // H
        EDGE_P = 0.01
        Bn, Nn, _ = h.shape
        qkv = h @ W
        qkv = qkv.reshape(Bn, Nn, 3, H, HEAD_DIM).transpose(2, 0, 3, 1, 4)
        q, k, v = (qkv[0], qkv[1], qkv[2])
        mask = jnp.where(adj == 0, -jnp.inf, 0.0)
        scores = jnp.einsum('bhid,bhjd->bhij', q, k) / np.sqrt(HEAD_DIM) + mask
        attn = jax.nn.softmax(scores, axis=-1)
        out = jnp.einsum('bhij,bhjd->bhid', attn, v)
        return out.transpose(0, 2, 1, 3).reshape(Bn, Nn, OUT_DIM)
    x = _layernorm(x + _L0_gnn_ref(x, adj, L0_gnn_alpha_train, L0_gnn_w, L0_gnn_d, L0_gnn_fc_in_w, L0_gnn_fc_in_b, 0), axis=-1)
    x = _layernorm(x + _L1_gnn_ref(x, L1_gnn_W, adj), axis=-1)
    return x

_drawn_inputs = setup_inputs


def setup_inputs(seed=0):
    import zlib

    import numpy as np

    out = dict(_drawn_inputs(seed))
    spreads = {'L0_gnn_alpha_train': (1.0, 0.2), 'L0_gnn_fc_in_b': (0.0, 0.1)}
    factors = {}
    for name, (base, spread) in spreads.items():
        noise = np.random.default_rng([zlib.crc32(name.encode()), seed]).standard_normal(out[name].shape)
        drawn = base * np.exp(spread * noise) if base else spread * noise
        out[name] = jnp.asarray(drawn.astype(out[name].dtype))
    for name, factor in factors.items():
        out[name] = (out[name] * factor).astype(out[name].dtype)
    return out
```

```python
from contextlib import ExitStack

import concourse.bass as bass
from concourse import mybir

F32 = mybir.dt.float32
F32R = mybir.dt.float32r
ALU = mybir.AluOpType
ACT = mybir.ActivationFunctionType

B, N, D = 16, 512, 128
P = 128
NT = N // P
GB = 4
NG = B // GB
STEPS = 8
DT = 1.0 / STEPS
H = 4
HD = D // H
SCALE = HD ** -0.5
EPS = 1e-5
NEG = -1e30
SLOT = D + 2
RS = STEPS + 1
VW = 2 * HD + 2
KS = 3 * HD

IPG = STEPS // 2
TPI = 2 * NT
PREP = IPG
ATT = IPG + 1
UPG = 2 * NT + IPG * TPI

EVENTS = [
    ("TR", 0, 0), ("TR", 0, 1), ("S", 1, 0), ("S", 1, 1), ("LN1", 0, 0), ("L0", 0, 0),
    ("TR", 0, 2), ("TR", 0, 3), ("S", 1, 2), ("S", 1, 3), ("X1T", 0, 0), ("L0", 1, 0),
    ("PV", 0, 0), ("TR", 1, 0), ("TR", 1, 1), ("S", 2, 0), ("S", 2, 1), ("Q", 0, 0), ("L0", 2, 0),
    ("K", 0, 0), ("TR", 1, 2), ("TR", 1, 3), ("S", 2, 2), ("S", 2, 3), ("CB", 0, 0), ("L0", 3, 0),
    ("PV", 1, 0), ("TR", 2, 0), ("TR", 2, 1), ("S", 3, 0), ("S", 3, 1), ("L0", 4, 0),
    ("TR", 2, 2), ("TR", 2, 3), ("S", 3, 2), ("S", 3, 3), ("CB", 1, 0), ("L0", 5, 0),
    ("PV", 2, 0), ("TR", 3, 0), ("TR", 3, 1), ("S0", 0, 0), ("S0", 0, 1), ("L0", 6, 0),
    ("TR", 3, 2), ("TR", 3, 3), ("S0", 0, 2), ("S0", 0, 3), ("CB", 2, 0), ("L0", 7, 0),
    ("PV", 3, 0), ("V", 0, 0), ("CB", 3, 0), ("LN2", 0, 0),
]
PREP_KINDS = ("LN1", "X1T", "Q", "K", "V", "S0")
ATT_KINDS = ("TR", "S", "PV", "CB", "LN2")
M_KINDS = ("X1T", "Q", "K", "V", "CB")


def events(horner, prep, att):
    m = 0
    for kind, a, b in EVENTS:
        if kind == "L0" and not horner or kind in PREP_KINDS and not prep or kind in ATT_KINDS and not att:
            continue
        yield kind, a, b, m
        m += kind in M_KINDS


M_FULL = sum(k in M_KINDS for k, _, _ in EVENTS)
M_PREP = sum(k in M_KINDS and k in PREP_KINDS for k, _, _ in EVENTS)


def m_base(it, first):
    return 0 if first else M_PREP + M_FULL * (it - ATT)


def carry_waits(eng, passed):
    eng.sem_inc(passed, 1)


def run_iterations(eng, boundary, iteration, unroll=False):
    boundary(0)
    with eng.Fori(0, IPG) as j:
        iteration(0, j, True, False, False)
    boundary(1)
    iteration(1, 0, True, True, False)
    with eng.Fori(1, IPG) as j:
        iteration(1, j, True, True, True)

    def middle(g):
        boundary(g)
        with eng.Fori(0, IPG) as j:
            iteration(g, j, True, True, True)

    if unroll:
        for g in range(2, NG):
            middle(g)
    else:
        with eng.Fori(2, NG) as g:
            middle(g)
    boundary(NG)
    with eng.Fori(0, IPG) as j:
        iteration(NG, j, False, True, True)
    iteration(NG + 1, 0, False, False, True)


def gnn_kernel(nc, x, adj, alpha, w, d, fc_w, fc_b, w_qkv, out):
    with ExitStack() as ctx:
        def sb(name, shape, dt=F32):
            return ctx.enter_context(nc.sbuf_tensor(name, shape, dt))

        def sem(name):
            return ctx.enter_context(nc.semaphore(name))

        ident = sb("ident", [P, P])
        decay_ident = sb("decay_ident", [P, P])
        ones = sb("ones", [P, P], F32R)
        fold = sb("fold", [P, HD + 2])
        pick = sb("pick", [P, RS])
        mask = sb("mask", [P, NT, N])
        PTh = sb("PTh", [P, NT, N], F32R)
        PTl = sb("PTl", [P, NT, N], F32R)
        Rh = sb("Rh", [P, RS, D], F32R)
        Rl = sb("Rl", [P, RS, D], F32R)
        rb = sb("rb", [P, RS, D], F32R)
        Wh = sb("Wh", [P, 3 * D], F32R)
        Wl = sb("Wl", [P, 3 * D], F32R)
        w_sb = sb("w_sb", [P, D])
        wT = sb("wT", [P, D])
        wdT = sb("wdT", [P, D])
        Qm = sb("Qm", [P, D])
        W_sb = sb("W_sb", [P, 3 * D])
        dcol = sb("dcol", [P, 1])
        dclip = sb("dclip", [P, 1])
        alph = sb("alph", [P, NT])
        rate = sb("rate", [P, NT])
        nrate = sb("nrate", [P, NT])
        bcols = sb("bcols", [P, 64])
        brow = sb("brow", [P, D], F32R)
        xin = sb("xin", [P, GB, NT, D])
        xTh = sb("xTh", [P, GB, N], F32R)
        xTl = sb("xTl", [P, GB, N], F32R)
        Yh = sb("Yh", [P, 2, NT, N], F32R)
        Yl = sb("Yl", [P, 2, NT, N], F32R)
        u = sb("u", [P, NT, N])
        x1 = sb("x1", [P, NT, D])
        x1res = sb("x1res", [P, NT, D])
        x1Th = sb("x1Th", [P, N], F32R)
        x1Tl = sb("x1Tl", [P, N], F32R)
        qh = sb("qh", [P, N], F32R)
        ql = sb("ql", [P, N], F32R)
        kh = sb("kh", [P, N], F32R)
        kl = sb("kl", [P, N], F32R)
        Qs = sb("Qs", [P, H, N], F32R)
        Ks = sb("Ks", [P, H, N], F32R)
        V = sb("V", [P, NT * H, VW], F32R)
        Sm = sb("Sm", [P, 2, N])
        negmax = sb("negmax", [P, H * NT])
        E = sb("E", [P, 2, NT, N])
        ETh = sb("ETh", [P, NT, N], F32R)
        ETl = sb("ETl", [P, NT, N], F32R)
        oT = sb("oT", [P, 2, N])
        rec = sb("rec", [P, NT])
        att = sb("att", [P, NT, D])
        y = sb("y", [P, NT, D])
        stats = sb("stats", [P, 2, NT, 6])
        mv = sb("mv", [P, 2, NT, 2])
        var = sb("var", [P, 2, NT])
        rstd = sb("rstd", [P, 2, NT])
        minus_half = sb("minus_half", [P, NT])
        Rst = sb("Rst", [P, 2, RS + 1, SLOT])
        Padj = E[:, 0, :, :]

        def bank(name):
            return ctx.enter_context(nc.psum_tensor(name, [P, N], F32))

        psL = [bank("psL0"), bank("psL1")]
        psS = [bank("psS0"), bank("psS1")]
        psE = [bank("psE0"), bank("psE1")]
        psO = bank("psO")
        psM = bank("psM")
        R_BANKS = [psL[0], psL[1], psO]

        in_w = sem("in_w")
        in_adj = sem("in_adj")
        in_fc = sem("in_fc")
        in_qkv = sem("in_qkv")
        c_ident = sem("c_ident")
        c_pool = sem("c_pool")
        dve_passed = sem("dve_passed")
        pool_passed = sem("pool_passed")
        c_pow = sem("c_pow")
        c_vec = sem("c_vec")
        c_act = sem("c_act")
        c_pe = sem("c_pe")
        xin_in = sem("xin_in")
        l0_mm = sem("l0_mm")
        l0_hi = sem("l0_hi")
        l0_lo = sem("l0_lo")
        u_sum = sem("u_sum")
        x1_done = sem("x1_done")
        x1_kept = sem("x1_kept")
        m_mm = sem("m_mm")
        m_hi = sem("m_hi")
        m_ev = sem("m_ev")
        stacked = [sem(f"stacked{h}") for h in range(H)]
        s_mm = sem("s_mm")
        s_max = sem("s_max")
        s_exp = sem("s_exp")
        t_mm = sem("t_mm")
        t_hi = sem("t_hi")
        t_lo = sem("t_lo")
        o_mm = sem("o_mm")
        o_ev = sem("o_ev")
        r_done = sem("r_done")
        z_done = sem("z_done")
        y_done = sem("y_done")
        y_out = sem("y_out")
        ln = [sem("ln1"), sem("ln2")]
        root = [sem("root1"), sem("root2")]
        T_FREE = 2
        O_FREE = 1
        Y_FREE = 16

        def f(ap):
            return ap.bitcast(F32)

        def unit0(it, g):
            return TPI * it + 2 * NT * (g + 1)

        def s_unit(a, h, i):
            return (a * H + h) * NT + i

        x_v = x.rearrange("b (t p) d -> p b t d", p=P)
        out_v = out.rearrange("b (t p) d -> p b t d", p=P)

        block = ctx.enter_context(nc.Block())

        @block.sync
        def _(sp):
            sp.dma_start(w_sb[:, :], w).then_inc(in_w, 16)
            sp.dma_start(dcol[:, :], d.rearrange("(p a) -> p a", a=1)).then_inc(in_w, 16)
            sp.dma_start(Rst[:, 0, 1, 0:D], fc_w).then_inc(in_fc, 16)
            sp.dma_start(Rst[:, 0, 1, D:D + 1], fc_b.rearrange("(p a) -> p a", a=1)).then_inc(in_fc, 16)
            sp.dma_start(Padj, adj.rearrange("(t p) m -> p t m", p=P)).then_inc(in_adj, 16)
            sp.dma_start(alph[:, :], alpha.rearrange("(t p) -> p t", p=P),
                         allow_slow_non_contiguous=True).then_inc(in_adj, 16)
            sp.dma_start(W_sb[:, :], w_qkv).then_inc(in_qkv, 16)
            sp.dma_start(xin[:, :, :, :], x_v[:, 0:GB]).then_inc(xin_in, 16)

            def boundary(g):
                if isinstance(g, int) and g >= NG - 1:
                    return
                sp.wait_ge(l0_mm, UPG * g + GB)
                sp.dma_start(xin[:, :, :, :], x_v[:, bass.ds((g + 1) * GB, GB)]).then_inc(xin_in, 16)

            def iteration(g, j, horner, prep, attend):
                it = g * IPG + j
                if prep:
                    first = not attend
                    k_at = next(m for kind, _, _, m in events(horner, prep, attend) if kind == "K")
                    sp.wait_ge(m_ev, m_base(it, first) + k_at + 1)
                    for h in range(H):
                        if attend:
                            sp.wait_ge(s_mm, s_unit(it - ATT, h, NT))
                        rows = slice(h * HD, (h + 1) * HD)
                        for r, (q, k) in enumerate(((qh, kh), (ql, kh), (qh, kl))):
                            at = slice(r * HD, (r + 1) * HD)
                            sp.dma_start(f(Qs[at, h, :]), f(q[rows, :])).then_inc(stacked[h], 16)
                            sp.dma_start(f(Ks[at, h, :]), f(k[rows, :])).then_inc(stacked[h], 16)
                if attend:
                    sp.wait_ge(y_done, it - ATT + 1)
                    sp.dma_start(out_v[:, bass.ds(it - ATT, 1)],
                                 y[:, :, :].rearrange("p (o t) d -> p o t d", o=1)).then_inc(y_out, 16)

            run_iterations(sp, boundary, iteration, unroll=True)
            sp.wait_ge(y_out, 16 * B + Y_FREE)

        @block.gpsimd
        def _(pool):
            nc.gpsimd.memset(ident[:, :], 0.0).then_inc(c_ident, 1)
            pool.wait_ge(c_ident, 1)
            nc.gpsimd.affine_select(out=ident[:, :], in_=ident[:, :], compare_op=ALU.not_equal, fill=1.0,
                                    base=0, pattern=[[-1, P]], channel_multiplier=1).then_inc(c_ident, 1)
            nc.gpsimd.memset(Rst[:, 1, 1:RS + 1, :], 0.0).then_inc(c_pool, 1)
            nc.gpsimd.memset(Rst[:, 0, 2:RS + 1, :], 0.0)
            nc.gpsimd.memset(Rst[:, 0, 1, D + 1:SLOT], 0.0).then_inc(c_pool, 1)
            nc.gpsimd.memset(Rst[:, :, 0, :], 0.0).then_inc(c_pool, 1)
            nc.gpsimd.memset(pick[:, :], 0.0).then_inc(c_pool, 1)
            nc.gpsimd.memset(bcols[:, :], 0.0).then_inc(c_pool, 1)
            nc.gpsimd.memset(f(rb[:, :, :]), 0.0).then_inc(c_pool, 1)
            nc.gpsimd.memset(f(ones[:, :]), 1.0).then_inc(c_pool, 1)
            nc.gpsimd.memset(f(V[:, :, 2 * HD:VW]), 1.0).then_inc(c_pool, 1)
            nc.gpsimd.memset(fold[:, :], 0.0).then_inc(c_pool, 1)
            nc.gpsimd.memset(minus_half[:, :], -0.5).then_inc(c_pow, 1)
            pool.wait_ge(c_pow, 1)
            pool.wait_ge(c_pool, 9)
            for half in range(2):
                nc.gpsimd.affine_select(out=pick[:, :], in_=pick[:, :], compare_op=ALU.not_equal, fill=1.0,
                                        base=-(RS - 1) - 32 * half, pattern=[[1, RS]],
                                        channel_multiplier=1).then_inc(c_pool, 1)
                pool.wait_ge(c_pool, 10 + half)
            for half in range(3):
                cols = slice(HD, HD + 1) if half == 2 else slice(0, HD)
                nc.gpsimd.affine_select(out=fold[:, cols], in_=fold[:, cols], compare_op=ALU.not_equal,
                                        fill=1.0, base=-HD * half, pattern=[[-1, cols.stop - cols.start]],
                                        channel_multiplier=1).then_inc(c_pool, 1)
                pool.wait_ge(c_pool, 12 + half)

            def boundary(g):
                if isinstance(g, int) and g == 0:
                    return
                for t in range(NT):
                    pool.wait_ge(l0_lo, UPG * g - NT + t + 1)
                    if t == 0:
                        pool.wait_ge(x1_done, (g - 1) * GB)
                    nc.gpsimd.tensor_tensor(u[:, t, :], f(Yh[:, 0, t, :]), f(Yl[:, 0, t, :]),
                                            ALU.add).then_inc(u_sum, 1)

            def inverse_root(which, count):
                pool.wait_ge(ln[which], 3 * count + 3)
                nc.gpsimd.tensor_tensor(rstd[:, which, :], var[:, which, :], minus_half[:, :],
                                        ALU.pow).then_inc(root[which], 1)

            def iteration(g, j, horner, prep, attend):
                it = g * IPG + j
                if prep:
                    batch = it - PREP
                    inverse_root(0, batch)
                    pool.wait_ge(x1_done, batch + 1)
                    pool.wait_ge(z_done, batch)
                    carry_waits(pool, pool_passed)
                    nc.gpsimd.tensor_copy(x1res[:, :, :], x1[:, :, :]).then_inc(x1_kept, 1)
                if attend:
                    inverse_root(1, it - ATT)

            run_iterations(pool, boundary, iteration)

        @block.scalar
        def _(act):
            act.wait_ge(in_adj, 32)
            nc.scalar.activation(rate[:, :], alph[:, :], ACT.Tanh, scale=0.5).then_inc(c_act, 1)
            act.wait_ge(in_qkv, 16)
            nc.scalar.activation(Wh[:, :], W_sb[:, :], ACT.Copy).then_inc(c_act, 1)
            for m in range(NT):
                act.wait_ge(c_pe, 2 + STEPS + 1 + m)
                nc.scalar.activation(PTh[:, m, :], (psS + psE)[m][:, :], ACT.Copy).then_inc(c_act, 1)
            for c in range(3):
                q0, q1 = 4 * c, min(4 * c + 4, RS)
                act.wait_ge(c_pe, 2 + STEPS + NT + 2 + c)
                nc.scalar.activation(Rh[:, q0:q1, :], R_BANKS[c][:, 0:(q1 - q0) * D].rearrange(
                    "p (q d) -> p q d", d=D), ACT.Copy).then_inc(c_act, 1)

            def high(bank_ap, dst):
                return nc.scalar.activation(dst, bank_ap, ACT.Copy)

            def boundary(g):
                if isinstance(g, int) and g == NG:
                    return
                for n in range(GB):
                    act.wait_ge(l0_mm, UPG * g + n + 1)
                    high(psL[n % 2][:, :], xTh[:, n, :]).then_inc(l0_hi, 1)
                for t in range(NT):
                    act.wait_ge(l0_mm, UPG * g + GB + t + 1)
                    if not isinstance(g, int) or g > 0:
                        act.wait_ge(u_sum, (g - 1) * NT + t + 1)
                    high(psL[t % 2][:, :], Yh[:, 0, t, :]).then_inc(l0_hi, 1)

            def exponential(a, h, i, fresh):
                s = s_unit(a, h, i)
                act.wait_ge(s_max, s + 1)
                if not fresh:
                    act.wait_ge(t_lo, s_unit(a, h - 1, 0) + T_FREE)
                nc.scalar.activation(E[:, h % 2, i, :], Sm[:, i % 2, :], ACT.Exp, scale=-1.0,
                                     bias=negmax[:, h * NT + i:h * NT + i + 1]).then_inc(s_exp, 1)

            def iteration(g, j, horner, prep, attend):
                it = g * IPG + j
                a, p = it - ATT, it - PREP
                hi = 0
                for kind, n, i, m in events(horner, prep, attend):
                    if kind == "L0":
                        act.wait_ge(l0_mm, unit0(it, g) + n + 1)
                        high(psL[n % 2][:, :], Yh[:, 1 - n // NT, n % NT, :]).then_inc(l0_hi, 1)
                    elif kind in ("X1T", "Q", "K", "V"):
                        act.wait_ge(m_mm, m_base(it, not attend) + m + 1)
                        if kind == "X1T":
                            dst, src = x1Th[:, :], psM[:, :]
                        elif kind == "V":
                            dst, src = V[:, :, 0:HD], psM[:, :].rearrange("p (a d) -> p a d", d=HD)
                        else:
                            dst, src = (qh if kind == "Q" else kh)[:, :], psM[:, :]
                            if kind == "Q":
                                for h in range(H):
                                    act.wait_ge(stacked[h], 6 * 16 * p)
                        high(src, dst).then_inc(m_hi, 1)
                    elif kind == "S":
                        exponential(a, n, i, False)
                    elif kind == "S0":
                        exponential(p, 0, i, not attend)
                    elif kind == "TR":
                        act.wait_ge(t_mm, s_unit(a, n, i) + 1)
                        high(psE[i % 2][:, :], ETh[:, i, :]).then_inc(t_hi, 1)
                    elif kind == "PV":
                        act.wait_ge(o_mm, a * H + n + 1)
                        nc.scalar.activation(oT[0:2 * HD + 1, n % 2, :], psO[0:2 * HD + 1, :],
                                             ACT.Copy).then_inc(o_ev, 1)

            run_iterations(act, boundary, iteration)

        @block.tensor
        def _(pe):
            mm = nc.tensor.matmul

            pe.wait_ge(c_ident, 2)
            pe.wait_ge(in_w, 32)
            nc.tensor.transpose(psM[:, 0:D], w_sb[:, :], ident[:, :]).then_inc(c_pe, 1)
            pe.wait_ge(c_vec, 3)
            mm(psM[:, 0:D], wdT[:, :], wT[:, :], start=True, stop=True).then_inc(c_pe, 1)
            pe.wait_ge(in_fc, 32)
            pe.wait_ge(c_pool, 3)
            for t in range(STEPS):
                pe.wait_ge(c_vec, 5 + t)
                for c in range(t // 3 + 1):
                    k0, k1 = 3 * c, min(3 * c + 3, t + 1)
                    last = mm(R_BANKS[c][:, 0:(k1 - k0) * SLOT], Qm[:, :],
                              Rst[:, t % 2, 1 + k0:1 + k1, :], start=True, stop=True)
                last.then_inc(c_pe, 1)
            pe.wait_ge(c_vec, 5 + STEPS + 1)
            for m in range(NT):
                for t in range(NT):
                    last = nc.tensor.transpose((psS + psE)[m][:, t * P:(t + 1) * P],
                                               Padj[:, t, m * P:(m + 1) * P], ident[:, :])
                last.then_inc(c_pe, 1)
            pe.wait_ge(c_vec, 5 + STEPS + 2)
            mm(psM[0:64, 0:D], bcols[:, :], ident[:, :], start=True, stop=True).then_inc(c_pe, 1)
            for c in range(3):
                for q in range(4 * c, min(4 * c + 4, RS)):
                    last = nc.tensor.transpose(R_BANKS[c][:, (q - 4 * c) * D:(q - 4 * c + 1) * D],
                                               Rst[:, STEPS % 2, RS - q, 0:D], ident[:, :])
                last.then_inc(c_pe, 1)
            pe.wait_ge(c_vec, 5 + STEPS + 10)

            def coefficient(bank_ap, q, t, alone):
                mm(bank_ap, ones[:, :], bcast_mid(rb[:, q, :]), start=True, stop=False)
                for b in range(GB):
                    cols = bank_ap[:, b * D:(b + 1) * D]
                    nodes = slice(t * P, (t + 1) * P)
                    mm(cols, xTh[:, b, nodes], Rh[:, q, :], start=False, stop=False)
                    mm(cols, xTh[:, b, nodes], Rl[:, q, :], start=False, stop=False)
                    last = mm(cols, xTl[:, b, nodes], Rh[:, q, :], start=False,
                              stop=alone and b == GB - 1)
                return last

            def bcast_mid(ap):
                return bass.AP(ap.tensor, ap.offset, [list(ap.ap[0]), [0, GB], list(ap.ap[-1])])

            def boundary(g):
                if isinstance(g, int) and g == NG:
                    return
                fresh = isinstance(g, int) and g == 0
                pe.wait_ge(xin_in, 16 * (g + 1))
                for b in range(GB):
                    if not fresh or b >= 2:
                        pe.wait_ge(l0_lo, UPG * g + b - 1)
                    for t in range(NT):
                        last = nc.tensor.transpose(psL[b % 2][:, t * P:(t + 1) * P],
                                                   xin[:, b, t, :], ident[:, :])
                    last.then_inc(l0_mm, 1)
                for t in range(NT):
                    pe.wait_ge(l0_lo, UPG * g + GB + t - (t > 0))
                    coefficient(psL[t % 2][:, :], slice(0, 1), t, True).then_inc(l0_mm, 1)

            def horner_tile(g, j, n):
                step, t = n // NT, n % NT
                unit = unit0(g * IPG + j, g) + n
                pe.wait_ge(l0_lo, unit - 1)
                coefficient(psL[n % 2][:, :], bass.ds(2 * j + 1 + step, 1), t, False)
                for k in range(NT):
                    if t == 0 and k == NT - 1:
                        pe.wait_ge(l0_lo, unit)
                    nodes = slice(t * P, (t + 1) * P)
                    mm(psL[n % 2][:, :], PTh[:, k, nodes], Yh[:, step, k, :], start=False, stop=False)
                    mm(psL[n % 2][:, :], PTh[:, k, nodes], Yl[:, step, k, :], start=False, stop=False)
                    last = mm(psL[n % 2][:, :], PTl[:, k, nodes], Yh[:, step, k, :],
                              start=False, stop=(k == NT - 1))
                last.then_inc(l0_mm, 1)

            def scores(a, h, i, fresh):
                s = s_unit(a, h, i)
                if i == 0:
                    pe.wait_ge(stacked[h], 6 * 16 * (a + 1))
                if not fresh or i >= 2:
                    pe.wait_ge(s_max, s - 1)
                mm(psS[i % 2][:, :], Qs[0:KS, h, i * P:(i + 1) * P], Ks[0:KS, h, :],
                   start=True, stop=True).then_inc(s_mm, 1)

            def iteration(g, j, horner, prep, attend):
                it = g * IPG + j
                a, p = it - ATT, it - PREP
                for kind, n, i, m in events(horner, prep, attend):
                    if kind in M_KINDS:
                        pe.wait_ge(m_ev, m_base(it, not attend) + m)
                    if kind == "L0":
                        horner_tile(g, j, n)
                    elif kind == "X1T":
                        pe.wait_ge(x1_done, p + 1)
                        for t in range(NT):
                            last = nc.tensor.transpose(psM[:, t * P:(t + 1) * P], x1[:, t, :], ident[:, :])
                        last.then_inc(m_mm, 1)
                    elif kind in ("Q", "K"):
                        cols = slice(0, D) if kind == "Q" else slice(D, 2 * D)
                        mm(psM[:, :], Wh[:, cols], x1Th[:, :], start=True, stop=False)
                        mm(psM[:, :], Wh[:, cols], x1Tl[:, :], start=False, stop=False)
                        mm(psM[:, :], Wl[:, cols], x1Th[:, :], start=False, stop=True).then_inc(m_mm, 1)
                    elif kind == "V":
                        cols = slice(2 * D, 3 * D)
                        for t in range(NT):
                            nodes = slice(t * P, (t + 1) * P)
                            mm(psM[:, nodes], x1Th[:, nodes], Wh[:, cols], start=True, stop=False)
                            mm(psM[:, nodes], x1Th[:, nodes], Wl[:, cols], start=False, stop=False)
                            last = mm(psM[:, nodes], x1Tl[:, nodes], Wh[:, cols], start=False, stop=True)
                        last.then_inc(m_mm, 1)
                    elif kind == "S":
                        scores(a, n, i, False)
                    elif kind == "S0":
                        scores(p, 0, i, not attend)
                    elif kind == "TR":
                        r = s_unit(a, n, i)
                        if i == 0:
                            pe.wait_ge(s_exp, s_unit(a, n, NT))
                        pe.wait_ge(t_lo, r - 1 + T_FREE)
                        for t in range(NT):
                            last = nc.tensor.transpose(psE[i % 2][:, t * P:(t + 1) * P],
                                                       E[:, n % 2, t, i * P:(i + 1) * P], ident[:, :])
                        last.then_inc(t_mm, 1)
                    elif kind == "PV":
                        pe.wait_ge(t_lo, s_unit(a, n, NT) + T_FREE)
                        pe.wait_ge(o_ev, a * H + n + O_FREE)
                        if n == 0:
                            pe.wait_ge(m_ev, m_base(it, False))
                        for t in range(NT):
                            for part in (ETh, ETl):
                                last = mm(psO[0:2 * HD + 1, :], V[:, t * H + n, 0:2 * HD + 1], part[:, t, :],
                                          start=(t == 0 and part is ETh), stop=(t == NT - 1 and part is ETl))
                        last.then_inc(o_mm, 1)
                    elif kind == "CB":
                        pe.wait_ge(o_ev, a * H + n + 1 + O_FREE)
                        for t in range(NT):
                            last = mm(psM[:, t * (HD + 1):(t + 1) * (HD + 1)],
                                      oT[0:2 * HD + 1, n % 2, t * P:(t + 1) * P],
                                      fold[0:2 * HD + 1, 0:HD + 1], start=True, stop=True)
                        last.then_inc(m_mm, 1)

            run_iterations(pe, boundary, iteration)

        @block.vector
        def _(dve):
            V_ = nc.vector

            dve.wait_ge(in_w, 32)
            V_.tensor_scalar(dclip[:, :], dcol[:, :], 0.0, 1.0, ALU.max, ALU.min).then_inc(c_vec, 1)
            dve.wait_ge(c_pe, 1)
            dve.wait_ge(c_vec, 1)
            V_.tensor_copy(wT[:, :], psM[:, 0:D]).then_inc(c_vec, 1)
            V_.tensor_scalar(wdT[:, :], psM[:, 0:D], dclip[:, 0:1], None, ALU.mult).then_inc(c_vec, 1)
            dve.wait_ge(c_ident, 2)
            dve.wait_ge(c_pool, 3)
            for par in range(2):
                V_.tensor_scalar(Rst[:, par, 0, 0:D], ident[:, :], DT, None, ALU.mult)
            V_.tensor_scalar(decay_ident[:, :], ident[:, :], 1.0 - DT, None, ALU.mult).then_inc(c_vec, 1)
            dve.wait_ge(c_vec, 4)
            dve.wait_ge(c_pe, 2)
            V_.scalar_tensor_tensor(out=Qm[:, :], in0=psM[:, 0:D], scalar=DT, in1=decay_ident[:, :],
                                    op0=ALU.mult, op1=ALU.add).then_inc(c_vec, 1)
            dve.wait_ge(in_fc, 32)
            for t in range(STEPS):
                old, new = t % 2, (t + 1) % 2
                dve.wait_ge(c_pe, 2 + t + 1)
                dve.wait_ge(c_vec, 5 + t)
                for c in range(t // 3 + 1):
                    k0, k1 = 3 * c, min(3 * c + 3, t + 1)
                    V_.tensor_tensor(Rst[:, new, 1 + k0:1 + k1, :],
                                     R_BANKS[c][:, 0:(k1 - k0) * SLOT].rearrange("p (k s) -> p k s", s=SLOT),
                                     Rst[:, old, k0:k1, :], ALU.add)
                V_.tensor_copy(Rst[:, new, 2 + t, :], Rst[:, old, 1 + t, :]).then_inc(c_vec, 1)
            done = 5 + STEPS
            dve.wait_ge(in_adj, 32)
            dve.wait_ge(c_act, 1)
            V_.tensor_scalar(mask[:, :, :], Padj, 0.0, NEG, ALU.is_equal, ALU.mult)
            V_.tensor_scalar(nrate[:, :], rate[:, :], -DT / 4, -DT / 4, ALU.mult, ALU.add)
            V_.tensor_scalar(rate[:, :], rate[:, :], DT / 4, DT / 4, ALU.mult, ALU.add).then_inc(r_done, 1)
            dve.wait_ge(r_done, 1)
            for t in range(NT):
                ins = V_.tensor_scalar(Padj[:, t, :], Padj[:, t, :], rate[:, t:t + 1], None, ALU.mult)
            ins.then_inc(r_done, 1)
            dve.wait_ge(r_done, 2)
            for t in range(NT):
                diag = Padj[:, t, t * P:(t + 1) * P]
                ins = V_.scalar_tensor_tensor(out=diag, in0=ident[:, :], scalar=nrate[:, t:t + 1], in1=diag,
                                              op0=ALU.mult, op1=ALU.add)
            ins.then_inc(c_vec, 1)
            done += 1
            dve.wait_ge(c_pool, 14)
            dve.wait_ge(c_vec, done - 1)
            last_r = Rst[:, STEPS % 2]
            for rows in (0, 32):
                V_.tensor_copy(bcols[:, rows:rows + RS], last_r[:, 1:1 + RS, D])
            V_.tensor_tensor(last_r[:, 1, 0:D], last_r[:, 1, 0:D], ident[:, :], ALU.add).then_inc(c_vec, 1)
            done += 1
            dve.wait_ge(c_act, 2)
            V_.tensor_tensor(Wl[:, :], W_sb[:, :], f(Wh[:, :]), ALU.subtract).then_inc(c_vec, 1)
            done += 1
            for m in range(NT):
                dve.wait_ge(c_act, 3 + m)
                ins = V_.tensor_tensor(PTl[:, m, :], (psS + psE)[m][:, :], f(PTh[:, m, :]), ALU.subtract)
            ins.then_inc(c_vec, 1)
            done += 1
            dve.wait_ge(c_pe, 2 + STEPS + NT + 1)
            V_.tensor_copy(brow[0:64, :], psM[0:64, 0:D]).then_inc(c_vec, 1)
            done += 1
            dve.wait_ge(c_vec, done)
            V_.tensor_tensor(brow[32:64, :], psM[32:64, 0:D], f(brow[32:64, :]), ALU.subtract).then_inc(c_vec, 1)
            done += 1
            dve.wait_ge(c_vec, done)
            for q in range(RS):
                ins = V_.tensor_scalar(rb[0:64, q, :], f(brow[0:64, :]), pick[0:64, q:q + 1], None, ALU.mult)
            ins.then_inc(c_vec, 1)
            done += 1
            for c in range(3):
                q0, q1 = 4 * c, min(4 * c + 4, RS)
                dve.wait_ge(c_act, 3 + NT + c)
                V_.tensor_tensor(Rl[:, q0:q1, :], R_BANKS[c][:, 0:(q1 - q0) * D].rearrange(
                    "p (q d) -> p q d", d=D), f(Rh[:, q0:q1, :]), ALU.subtract).then_inc(c_vec, 1)
                done += 1
            assert done == 5 + STEPS + 10, done
            V_.memset(rec[:, :], 0.0).then_inc(t_lo, T_FREE)
            V_.memset(y[:, :, :], 0.0).then_inc(y_out, Y_FREE)
            V_.memset(negmax[:, :], 0.0).then_inc(o_ev, O_FREE)

            def low(bank_ap, hi, dst):
                return V_.tensor_tensor(dst, bank_ap, f(hi), ALU.subtract)

            def boundary(g):
                if isinstance(g, int) and g == NG:
                    return
                for n in range(GB):
                    dve.wait_ge(l0_hi, UPG * g + n + 1)
                    low(psL[n % 2][:, :], xTh[:, n, :], xTl[:, n, :]).then_inc(l0_lo, 1)
                for t in range(NT):
                    dve.wait_ge(l0_hi, UPG * g + GB + t + 1)
                    low(psL[t % 2][:, :], Yh[:, 0, t, :], Yl[:, 0, t, :]).then_inc(l0_lo, 1)

            def layernorm(which, count, src, dst, before_write):
                s = ln[which]
                for t in range(NT):
                    ins = V_.bn_stats(stats[:, which, t, :], src(t))
                ins.then_inc(s, 1)
                dve.wait_ge(s, 3 * count + 1)
                carry_waits(dve, dve_passed)
                for t in range(NT):
                    ins = V_.bn_aggr(mv[:, which, t, :], stats[:, which, t, :])
                ins.then_inc(s, 1)
                dve.wait_ge(s, 3 * count + 2)
                V_.tensor_scalar(var[:, which, :], mv[:, which, :, 1], EPS, None, ALU.add).then_inc(s, 1)
                dve.wait_ge(root[which], count + 1)
                before_write()
                for t in range(NT):
                    ins = V_.tensor_scalar(dst[:, t, :], src(t), mv[:, which, t, 0:1],
                                           rstd[:, which, t:t + 1], ALU.subtract, ALU.mult)
                return ins

            def maximum(a, h, i, fresh):
                s = s_unit(a, h, i)
                at = h * NT + i
                dve.wait_ge(s_mm, s + 1)
                if not fresh or i >= 2:
                    dve.wait_ge(s_exp, s - 1)
                carry_waits(dve, dve_passed)
                V_.tensor_tensor_reduce(out=Sm[:, i % 2, :], in0=psS[i % 2][:, :], in1=mask[:, i, :],
                                        scale=-SCALE, scalar=3e38, op0=ALU.add, op1=ALU.min,
                                        accum_out=negmax[:, at:at + 1]).then_inc(s_max, 1)

            def iteration(g, j, horner, prep, attend):
                it = g * IPG + j
                a, p = it - ATT, it - PREP
                hi = 0
                for kind, n, i, m in events(horner, prep, attend):
                    if kind == "L0":
                        dve.wait_ge(l0_hi, unit0(it, g) + n + 1)
                        to = 1 - n // NT
                        low(psL[n % 2][:, :], Yh[:, to, n % NT, :], Yl[:, to, n % NT, :]).then_inc(l0_lo, 1)
                    elif kind == "LN1":
                        dve.wait_ge(u_sum, g * NT)

                        def x1_free():
                            dve.wait_ge(x1_kept, p)

                        layernorm(0, p, lambda t: u[:, t, bass.ds(j * D, D)], x1, x1_free).then_inc(x1_done, 1)
                    elif kind in ("X1T", "Q", "K", "V"):
                        hi += 1
                        dve.wait_ge(m_hi, 4 * p + hi)
                        if kind == "V":
                            low(psM[:, :].rearrange("p (a d) -> p a d", d=HD), V[:, :, 0:HD],
                                V[:, :, HD:2 * HD]).then_inc(m_ev, 1)
                        else:
                            h_, l_ = {"X1T": (x1Th, x1Tl), "Q": (qh, ql), "K": (kh, kl)}[kind]
                            low(psM[:, :], h_[:, :], l_[:, :]).then_inc(m_ev, 1)
                    elif kind == "S":
                        maximum(a, n, i, False)
                    elif kind == "S0":
                        maximum(p, 0, i, not attend)
                    elif kind == "TR":
                        dve.wait_ge(t_hi, s_unit(a, n, i) + 1)
                        low(psE[i % 2][:, :], ETh[:, i, :], ETl[:, i, :]).then_inc(t_lo, 1)
                    elif kind == "CB":
                        o = psM[:, 0:NT * (HD + 1)].rearrange("p (t c) -> p t c", c=HD + 1)
                        dve.wait_ge(m_mm, m_base(it, False) + m + 1)
                        V_.reciprocal(rec[:, :], o[:, :, HD]).then_inc(r_done, 1)
                        dve.wait_ge(r_done, 2 + a * H + n + 1)
                        r_b = bass.AP(rec, 0, [list(rec[:, :].ap[0]), [1, NT], [0, HD]])
                        V_.tensor_tensor(att[:, :, n * HD:(n + 1) * HD], o[:, :, 0:HD], r_b,
                                         ALU.mult).then_inc(m_ev, 1)
                    elif kind == "LN2":
                        dve.wait_ge(m_ev, m_base(it, False) + m)
                        dve.wait_ge(x1_kept, a + 1)
                        V_.tensor_tensor(att[:, :, :], att[:, :, :], x1res[:, :, :], ALU.add).then_inc(z_done, 1)
                        dve.wait_ge(z_done, a + 1)

                        def y_free():
                            dve.wait_ge(y_out, 16 * a + Y_FREE)

                        layernorm(1, a, lambda t: att[:, t, :], y, y_free).then_inc(y_done, 1)

            run_iterations(dve, boundary, iteration)


_INS = ["x", "adj", "L0_gnn_alpha_train", "L0_gnn_w", "L0_gnn_d", "L0_gnn_fc_in_w", "L0_gnn_fc_in_b", "L1_gnn_W"]


def kernel(**inputs):
    import numpy as _np
    import concourse.bacc as _bacc
    from concourse import mybir as _mybir
    from concourse.bass_utils import run_bass_kernel_spmd as _run

    nc = _bacc.Bacc("TRN2", target_bir_lowering=False, num_devices=1)
    arrays, args = {}, []
    for name in _INS:
        a = _np.ascontiguousarray(inputs[name])
        arrays[f"in_{name}_dram"] = a
        args.append(nc.dram_tensor(f"in_{name}_dram", a.shape, _mybir.dt.from_np(a.dtype), kind="ExternalInput").ap())
    args.append(nc.dram_tensor("out_0_dram", (B, N, D), _mybir.dt.float32, kind="ExternalOutput").ap())
    gnn_kernel(nc, *args)
    r = _run(nc, [arrays], core_ids=[0])
    return r.results[0]["out_0_dram"]
```

```python
from contextlib import ExitStack

import concourse.bass as bass
from concourse import mybir

F32 = mybir.dt.float32
F32R = mybir.dt.float32r
ALU = mybir.AluOpType
ACT = mybir.ActivationFunctionType

B, N, D = 16, 512, 128
P = 128
NT = N // P
GB = 2
GD = GB * D
TU = N // GD
UPS = NT // TU
NG = B // GB
STEPS = 8
DT = 1.0 / STEPS
H = 4
HD = D // H
SCALE = HD ** -0.5
EPS = 1e-5
NEG = -1e30
SLOT = D + 2
RS = STEPS + 1
PW = 3
BLK = RS // PW
QUAD = 32
VW = 4 * HD
KS = 3 * HD

IPG = GB
PREP = IPG
ATT = IPG + 1
END = IPG + 2
U_X, U_Z, U_C = 0, GB, PW * GB
U_B = U_C + UPS
UPG = U_B + (BLK - 1) * UPS
EPB = UPG // 2

EVENTS = [
    ("HORNER", 0, 0), ("TR", 0, 0), ("TR", 0, 1), ("S", 1, 0), ("S", 1, 1), ("CBF", 1, 0), ("LN1A", 0, 0),
    ("HORNER", 1, 0),
    ("TR", 0, 2), ("TR", 0, 3), ("S", 1, 2), ("S", 1, 3), ("LN2A", 0, 0), ("LN1B", 0, 0),
    ("HORNER", 2, 0), ("PV", 0, 0),
    ("TR", 1, 0), ("TR", 1, 1), ("S", 2, 0), ("S", 2, 1), ("LN2B", 0, 0),
    ("HORNER", 3, 0), ("X1T", 0, 0), ("X1L", 0, 0),
    ("TR", 1, 2), ("TR", 1, 3), ("S", 2, 2), ("S", 2, 3),
    ("HORNER", 4, 0), ("Q", 1, 0), ("QL", 1, 0), ("PV", 1, 0),
    ("TR", 2, 0), ("TR", 2, 1), ("S", 3, 0), ("S", 3, 1), ("K", 2, 0), ("KL", 2, 0),
    ("HORNER", 5, 0), ("CB", 0, 0),
    ("TR", 2, 2), ("TR", 2, 3), ("S", 3, 2), ("S", 3, 3),
    ("HORNER", 6, 0), ("PV", 2, 0),
    ("TR", 3, 0), ("TR", 3, 1), ("S0", 0, 0), ("S0", 0, 1),
    ("HORNER", 7, 0),
    ("TR", 3, 2), ("TR", 3, 3), ("S0", 0, 2), ("S0", 0, 3),
    ("HORNER", 8, 0), ("V", 3, 0), ("VL", 3, 0), ("PV", 3, 0),
]
LATE_EVENTS = [
    ("LN1A", 0, 0), ("TR", 0, 0), ("TR", 0, 1), ("TR", 0, 2), ("TR", 0, 3),
    ("S", 1, 0), ("S", 1, 1), ("CBF", 1, 0), ("S", 1, 2), ("S", 1, 3), ("LN2A", 0, 0), ("LN1B", 0, 0),
    ("TR", 1, 0), ("TR", 1, 1), ("TR", 1, 2), ("TR", 1, 3),
    ("S", 2, 0), ("S", 2, 1), ("X1T", 0, 0), ("PV", 0, 0), ("S", 2, 2), ("S", 2, 3),
    ("X1L", 0, 0), ("LN2B", 0, 0), ("Q", 1, 0),
    ("TR", 2, 0), ("TR", 2, 1), ("QL", 1, 0), ("TR", 2, 2), ("TR", 2, 3),
    ("S", 3, 0), ("K", 2, 0), ("S", 3, 1), ("PV", 1, 0), ("S", 3, 2), ("KL", 2, 0), ("S", 3, 3), ("CB", 0, 0),
    ("TR", 3, 0), ("TR", 3, 1), ("TR", 3, 2), ("TR", 3, 3),
    ("S0", 0, 0), ("S0", 0, 1), ("PV", 2, 0), ("V", 3, 0), ("S0", 0, 2), ("S0", 0, 3), ("VL", 3, 0),
    ("PV", 3, 0),
]
HORNER = [
    [[("XS", 0), ("XS", 1)], [("XT", 0), ("XT", 1)], [("Z", 0)], [("Z", 1)], [("Z", 2)], [("Z", 3)],
     [("C", 0)], [("C", 1)], [("BC", 0)]],
    [[], [("BM", 0)], [("BC", 1)], [("BM", 1)], [("BC", 2)], [("BM", 2)], [("BC", 3)], [("BM", 3)], []],
]
PREP_KINDS = ("LN1A", "LN1B", "X1T", "X1L", "Q", "QL", "K", "KL", "V", "VL", "S0")
ATT_KINDS = ("TR", "S", "PV", "CB")
END_KINDS = ("CBF", "LN2A", "LN2B")
MPB = 4


def events(j, horner, prep, att, end):
    for kind, n, i in EVENTS if horner or not att else LATE_EVENTS:
        if kind == "HORNER":
            for piece, m in HORNER[j][n] if horner else ():
                yield piece, m, 0
        elif prep and kind in PREP_KINDS or att and kind in ATT_KINDS or end and kind in END_KINDS:
            yield kind, n, i


def run_iterations(eng, iteration, last_apart=False):
    for j in range(IPG):
        iteration(0, j, True, False, False, False)
    for j in range(IPG):
        iteration(1, j, True, True, j > 0, False)
    with eng.Fori(2, NG - last_apart) as g:
        for j in range(IPG):
            iteration(g, j, True, True, True, True)
    if last_apart:
        for j in range(IPG):
            iteration(NG - 1, j, True, True, True, True)
    for j in range(IPG):
        iteration(NG, j, False, True, True, True)
    iteration(NG + 1, 0, False, False, True, True)
    iteration(NG + 1, 1, False, False, False, True)


def carry_waits(eng, passed):
    eng.sem_inc(passed, 1)


def gnn_kernel(nc, x, adj, alpha, w, d, fc_w, fc_b, w_qkv, out):
    with ExitStack() as ctx:
        def sb(name, shape, dt=F32):
            return ctx.enter_context(nc.sbuf_tensor(name, shape, dt))

        def sem(name):
            return ctx.enter_context(nc.semaphore(name))

        ident = sb("ident", [P, P])
        fold = sb("fold", [P, 2 * HD])
        mask = sb("mask", [P, NT, N])
        PTh = sb("PTh", [P, PW, NT, N], F32R)
        PTl = sb("PTl", [P, PW, NT, N], F32R)
        R = sb("R", [P, RS, D])
        rb = sb("rb", [P, BLK, D], F32R)
        Wst = sb("Wst", [P, N], F32R)
        sel = sb("sel", [P, PW, P], F32R)
        spread = sb("spread", [P, D], F32R)
        Wh = sb("Wh", [P, 3 * D], F32R)
        Wl = sb("Wl", [P, 3 * D], F32R)
        dcol = sb("dcol", [P, 1])
        dclip = sb("dclip", [P, 1])
        alph = sb("alph", [P, NT])
        rate = sb("rate", [P, NT])
        nrate = sb("nrate", [P, NT])
        xin = sb("xin", [P, GB, NT, D])
        Xh = sb("Xh", [P, GB, NT, D], F32R)
        Xl = sb("Xl", [P, GB, NT, D], F32R)
        zT = sb("zT", [P, PW, GB, N])
        Yh = sb("Yh", [P, 2, NT, GD], F32R)
        Yl = sb("Yl", [P, 2, NT, GD], F32R)
        u = sb("u", [P, NT, GD])
        x1 = sb("x1", [P, 2, NT, D])
        x1Th = sb("x1Th", [P, N], F32R)
        x1Tl = sb("x1Tl", [P, N], F32R)
        qh = sb("qh", [P, N], F32R)
        ql = sb("ql", [P, N], F32R)
        kh = sb("kh", [P, N], F32R)
        kl = sb("kl", [P, N], F32R)
        Qs = sb("Qs", [P, H, N], F32R)
        Ks = sb("Ks", [P, H, N], F32R)
        V = sb("V", [P, 2, NT, H // 2, 2, VW], F32R)
        w_sb, wT, wdT, Qm = (x1[:, 0, t, :] for t in range(4))
        decay_ident = x1[:, 1, 3, :]
        bcols = bass.AP(x1, NT * D, [list(x1[:, 0, 0, :].ap[0]), [3 * QUAD, BLK], [1, 3 * QUAD]])
        Sm = sb("Sm", [P, 2, N])
        W_sb = Sm[:, 0, 0:3 * D]
        negmax = sb("negmax", [P, H * NT])
        E = sb("E", [P, 2, NT, N])
        ETh = sb("ETh", [P, NT, N], F32R)
        ETl = sb("ETl", [P, NT, N], F32R)
        oT = sb("oT", [P, 2, N])
        sums = sb("sums", [P, H * NT])
        rec = sb("rec", [P, 2 * NT])
        att = sb("att", [P, NT, D])
        y = sb("y", [P, NT, D])
        stats = sb("stats", [P, 2, NT, 6])
        mv = sb("mv", [P, 2, NT, 2])
        var = sb("var", [P, 2, NT])
        rstd = sb("rstd", [P, 2, NT])
        minus_half = sb("minus_half", [P, NT])
        Rst = bass.AP(zT, 0, [list(zT[:, 0, 0, :].ap[0]), [(RS + 1) * SLOT, 2], [SLOT, RS + 1], [1, SLOT]])
        P_sb = E[:, 0, :, :]
        adj_sb = E[:, 1, :, :]
        Ph, Pl = ETh, ETl

        def bank(name):
            return ctx.enter_context(nc.psum_tensor(name, [P, N], F32))

        psL = [bank("psL0"), bank("psL1")]
        psS = [bank("psS0"), bank("psS1")]
        psE = [bank("psE0"), bank("psE1")]
        psO = bank("psO")
        psM = bank("psM")
        R_BANKS = [psL[0], psL[1], psO]
        P_BANKS = psS + psE

        in_w = sem("in_w")
        in_adj = sem("in_adj")
        in_fc = sem("in_fc")
        in_qkv = sem("in_qkv")
        in_alpha = sem("in_alpha")
        c_ident = sem("c_ident")
        c_pool = sem("c_pool")
        dve_passed = sem("dve_passed")
        pool_passed = sem("pool_passed")
        c_pow = sem("c_pow")
        c_vec = sem("c_vec")
        c_act = sem("c_act")
        c_pe = sem("c_pe")
        rec_mm = sem("rec_mm")
        rec_ev = sem("rec_ev")
        p_sb = sem("p_sb")
        p_hi = sem("p_hi")
        p_lo = sem("p_lo")
        pt_mm = sem("pt_mm")
        pt_hi = sem("pt_hi")
        pt_lo = sem("pt_lo")
        rt_mm = sem("rt_mm")
        rt_ev = sem("rt_ev")
        bias_in = sem("bias_in")
        bias_mm = sem("bias_mm")
        bias_hi = sem("bias_hi")
        bias_lo = sem("bias_lo")
        xin_in = sem("xin_in")
        l0_mm = sem("l0_mm")
        l0_hi = sem("l0_hi")
        l0_ev = [sem("l0_ev0"), sem("l0_ev1")]
        x_high = sem("x_high")
        x_split = sem("x_split")
        x1_done = sem("x1_done")
        m_mm = sem("m_mm")
        m_hi = sem("m_hi")
        m_ev = sem("m_ev")
        stacked = [sem(f"stacked{h}") for h in range(H)]
        s_mm = sem("s_mm")
        s_max = sem("s_max")
        s_exp = sem("s_exp")
        t_mm = sem("t_mm")
        t_hi = sem("t_hi")
        t_lo = sem("t_lo")
        o_mm = sem("o_mm")
        o_ev = sem("o_ev")
        c_mm = sem("c_mm")
        c_ev = sem("c_ev")
        r_done = sem("r_done")
        z_done = sem("z_done")
        y_done = sem("y_done")
        y_out = sem("y_out")
        ln = [sem("ln1"), sem("ln2")]
        root = [sem("root1"), sem("root2")]
        T_FREE = 2
        C_FREE = 1
        Y_FREE = 16

        def f(ap):
            return ap.bitcast(F32)

        def e_bank(horner, i):
            return psE[i % 2] if horner else (psE + psL)[i]

        def et(horner, h):
            return (Yh, Yl) if not horner and h % 2 else (ETh, ETl)

        def et_block(part, i):
            return bass.AP(part, i * N, [[NT * N, P], [1, N]])

        def units(n):
            return slice(n * TU, (n + 1) * TU)

        def v_part(bank_ap, e):
            return bank_ap[:, :].rearrange("p (t b e d) -> p t b e d", b=H // 2, e=2, d=HD)[:, :, :, e, :]

        def s_unit(a, h, i):
            return (a * H + h) * NT + i

        x_v = x.rearrange("b (t p) d -> p b t d", p=P)
        out_v = out.rearrange("b (t p) d -> p b t d", p=P)

        block = ctx.enter_context(nc.Block())

        @block.sync
        def _(sp):
            sp.dma_start(w_sb[:, :], w).then_inc(in_w, 16)
            sp.dma_start(dcol[:, :], d.rearrange("(p a) -> p a", a=1)).then_inc(in_w, 16)
            sp.dma_start(alph[:, :], alpha.rearrange("(t p) -> p t", p=P),
                         allow_slow_non_contiguous=True).then_inc(in_alpha, 16)
            sp.dma_start(adj_sb, adj.rearrange("(t p) m -> p t m", p=P)).then_inc(in_adj, 16)
            sp.dma_start(Rst[:, 0, 1, 0:D], fc_w).then_inc(in_fc, 16)
            sp.dma_start(Rst[:, 0, 1, D:D + 1], fc_b.rearrange("(p a) -> p a", a=1)).then_inc(in_fc, 16)
            sp.dma_start(W_sb[:, :], w_qkv).then_inc(in_qkv, 16)
            sp.dma_start(xin[:, :, :, :], x_v[:, 0:GB]).then_inc(xin_in, 16)

            def iteration(g, j, horner, prep, attend, end):
                it = g * IPG + j
                if horner and j == 0 and not (isinstance(g, int) and g == NG - 1):
                    sp.wait_ge(l0_mm, UPG * g + GB)
                    sp.wait_ge(x_split, (g + 1) * GB)
                    sp.dma_start(xin[:, :, :, :], x_v[:, bass.ds((g + 1) * GB, GB)]).then_inc(xin_in, 16)
                if end:
                    sp.wait_ge(y_done, it - END + 1)
                    sp.dma_start(out_v[:, bass.ds(it - END, 1)],
                                 y[:, :, :].rearrange("p (o t) d -> p o t d", o=1)).then_inc(y_out, 16)
                if prep:
                    sp.wait_ge(m_ev, MPB * (it - PREP) + 3)
                    for h in range(H):
                        if attend:
                            sp.wait_ge(s_mm, s_unit(it - ATT, h, NT))
                        rows = slice(h * HD, (h + 1) * HD)
                        for r, (q, k) in enumerate(((qh, kh), (ql, kh), (qh, kl))):
                            at = slice(r * HD, (r + 1) * HD)
                            sp.dma_start(f(Qs[at, h, :]), f(q[rows, :])).then_inc(stacked[h], 16)
                            sp.dma_start(f(Ks[at, h, :]), f(k[rows, :])).then_inc(stacked[h], 16)

            run_iterations(sp, iteration, last_apart=True)
            sp.wait_ge(y_out, 16 * B + Y_FREE)

        @block.gpsimd
        def _(pool):
            nc.gpsimd.memset(ident[:, :], 0.0).then_inc(c_ident, 1)
            pool.wait_ge(c_ident, 1)
            nc.gpsimd.affine_select(out=ident[:, :], in_=ident[:, :], compare_op=ALU.not_equal, fill=1.0,
                                    base=0, pattern=[[-1, P]], channel_multiplier=1).then_inc(c_ident, 1)
            nc.gpsimd.memset(Rst[:, 1, 1:RS + 1, :], 0.0).then_inc(c_pool, 1)
            nc.gpsimd.memset(Rst[:, 0, 2:RS + 1, :], 0.0)
            nc.gpsimd.memset(Rst[:, 0, 1, D + 1:SLOT], 0.0).then_inc(c_pool, 1)
            nc.gpsimd.memset(Rst[:, :, 0, :], 0.0).then_inc(c_pool, 1)
            nc.gpsimd.memset(bcols[:, :, :], 0.0).then_inc(c_pool, 1)
            nc.gpsimd.memset(f(sel[:, :, :]), 0.0).then_inc(c_pool, 1)
            nc.gpsimd.memset(fold[:, :], 0.0).then_inc(c_pool, 1)
            nc.gpsimd.memset(f(spread[:, :]), 1.0 / P).then_inc(c_pool, 1)
            nc.gpsimd.memset(minus_half[:, :], -0.5).then_inc(c_pow, 1)
            pool.wait_ge(c_pow, 1)
            pool.wait_ge(c_pool, 7)
            for i in range(PW):
                nc.gpsimd.memset(f(sel[:, i, :]).rearrange("p (h r) -> p h r", r=QUAD)[:, 0:3, i:RS:PW],
                                 1.0).then_inc(c_pool, 1)
            for t in range(NT):
                pool.wait_ge(p_hi, t + 1)
                nc.gpsimd.tensor_tensor(Pl[:, t, :], P_sb[:, t, :], f(Ph[:, t, :]),
                                        ALU.subtract).then_inc(p_lo, 1)
            for half in range(4):
                cols = slice(half // 2 * HD, (half // 2 + 1) * HD)
                nc.gpsimd.affine_select(out=fold[:, cols], in_=fold[:, cols], compare_op=ALU.not_equal,
                                        fill=1.0, base=-HD * half, pattern=[[-1, HD]],
                                        channel_multiplier=1).then_inc(c_pool, 1)
                pool.wait_ge(c_pool, 11 + half)
            nc.gpsimd.memset(f(V[:, :, :, :, :, :]), 0.0).then_inc(c_pool, 1)

            def inverse_root(which, count):
                pool.wait_ge(ln[which], 3 * count + 3)
                nc.gpsimd.tensor_tensor(rstd[:, which, :], var[:, which, :], minus_half[:, :],
                                        ALU.pow).then_inc(root[which], 1)

            def iteration(g, j, horner, prep, attend, end):
                it = g * IPG + j
                if horner and j == 0:
                    for b in range(GB):
                        pool.wait_ge(x_high, g * GB + b + 1)
                        nc.gpsimd.tensor_tensor(Xl[:, b], xin[:, b], f(Xh[:, b]),
                                                ALU.subtract).then_inc(x_split, 1)
                if not prep and end:
                    inverse_root(1, it - END)
                elif prep and end:
                    inverse_root(0, it - PREP)
                    inverse_root(1, it - END)
                elif prep:
                    inverse_root(0, it - PREP)

            run_iterations(pool, iteration)

        @block.scalar
        def _(act):
            act.wait_ge(in_alpha, 16)
            nc.scalar.activation(rate[:, :], alph[:, :], ACT.Tanh, scale=0.5).then_inc(c_act, 1)
            for t in range(NT):
                act.wait_ge(p_sb, t + 1)
                nc.scalar.activation(Ph[:, t, :], P_sb[:, t, :], ACT.Copy).then_inc(p_hi, 1)

            def power_high(i, m):
                act.wait_ge(pt_mm, i * NT + m + 1)
                nc.scalar.activation(PTh[:, i, m, :], P_BANKS[m][:, :], ACT.Copy).then_inc(pt_hi, 1)

            for i in range(PW - 1):
                for m in range(NT):
                    power_high(i, m)
            def split_x(g, b):
                if b == 0:
                    act.wait_ge(xin_in, 16 * (g + 1))
                nc.scalar.activation(Xh[:, b], xin[:, b], ACT.Copy).then_inc(x_high, 1)

            power_high(2, 0)
            for b in range(GB):
                split_x(0, b)
            power_high(2, 1)
            act.wait_ge(in_qkv, 16)
            nc.scalar.activation(Wh[:, :], W_sb[:, :], ACT.Copy).then_inc(c_act, 1)
            power_high(2, 2)
            act.wait_ge(bias_mm, 1)
            nc.scalar.activation(rb[0:3 * QUAD, :, :], psM[0:3 * QUAD, 0:BLK * D].rearrange(
                "p (q d) -> p q d", d=D), ACT.Copy).then_inc(bias_hi, 1)
            for c in range(3):
                q0, q1 = 4 * c, min(4 * c + 4, RS)
                act.wait_ge(rt_mm, c + 1)
                nc.scalar.activation(R[:, q0:q1, :], R_BANKS[c][:, 0:(q1 - q0) * D].rearrange(
                    "p (q d) -> p q d", d=D), ACT.Copy).then_inc(rt_ev, 1)
            power_high(2, 3)
            act.wait_ge(bias_mm, 2)
            nc.scalar.activation(Wst[0:3 * QUAD, :], psM[0:3 * QUAD, :], ACT.Copy).then_inc(bias_hi, 1)

            def high(bank_ap, dst):
                return nc.scalar.activation(dst, bank_ap, ACT.Copy)

            def exponential(a, h, i, fresh):
                s = s_unit(a, h, i)
                act.wait_ge(s_max, s + 1)
                if not fresh:
                    act.wait_ge(t_lo, s_unit(a, h - 1, 0) + T_FREE)
                nc.scalar.activation(E[:, h % 2, i, :], Sm[:, i % 2, :], ACT.Exp, scale=-1.0,
                                     bias=negmax[:, h * NT + i:h * NT + i + 1],
                                     accum_out=sums[:, h * NT + i:h * NT + i + 1]).then_inc(s_exp, 1)

            def iteration(g, j, horner, prep, attend, end):
                it = g * IPG + j
                a, p, e = it - ATT, it - PREP, it - END
                for kind, n, i in events(j, horner, prep, attend, end):
                    if kind == "XS":
                        if not isinstance(g, int) or g > 0:
                            split_x(g, n)
                    elif kind in ("XT", "Z"):
                        act.wait_ge(l0_mm, UPG * g + (U_Z if kind == "Z" else U_X) + n + 1)
                        power = 0 if kind == "XT" else n // GB + 1
                        nc.scalar.activation(zT[:, power, n % GB, :], psL[n % 2][:, :],
                                             ACT.Copy).then_inc(l0_ev[n % 2], 1)
                    elif kind == "C":
                        act.wait_ge(l0_mm, UPG * g + U_C + n + 1)
                        high(psL[n % 2][:, :], Yh[:, 0, units(n), :]).then_inc(l0_hi, 1)
                    elif kind == "BM":
                        act.wait_ge(l0_mm, UPG * g + U_B + n + 1)
                        if n < (BLK - 2) * UPS:
                            high(psL[n % 2][:, :], Yh[:, 1, units(n), :]).then_inc(l0_hi, 1)
                        else:
                            if not isinstance(g, int) or g > 0:
                                act.wait_ge(x1_done, g * GB)
                            nc.scalar.activation(u[:, units(n % UPS), :], psL[n % 2][:, :],
                                                 ACT.Copy).then_inc(l0_ev[n % 2], 1)
                    elif kind in ("X1T", "Q", "K", "V"):
                        act.wait_ge(m_mm, MPB * p + n + 1)
                        if kind == "V":
                            for e_ in range(2):
                                ins = high(v_part(psM, e_), V[:, j, :, :, e_, 2 * HD * e_:2 * HD * e_ + HD])
                            ins.then_inc(m_hi, 1)
                            continue
                        if kind == "Q":
                            for h in range(H):
                                act.wait_ge(stacked[h], 6 * 16 * p)
                        dst = {"X1T": x1Th, "Q": qh, "K": kh}[kind]
                        high(psM[:, :], dst[:, :]).then_inc(m_hi, 1)
                    elif kind == "S":
                        exponential(a, n, i, False)
                    elif kind == "S0":
                        exponential(p, 0, i, not attend)
                    elif kind == "TR":
                        act.wait_ge(t_mm, s_unit(a, n, i) + 1)
                        high(e_bank(horner, i)[:, :], et_block(et(horner, n)[0], i)).then_inc(t_hi, 1)
                    elif kind == "PV" and n % 2 == 1:
                        act.wait_ge(o_mm, a * 2 + n // 2 + 1)
                        nc.scalar.activation(oT[:, n // 2, :], psO[:, :], ACT.Copy).then_inc(o_ev, 1)

            run_iterations(act, iteration)

        @block.tensor
        def _(pe):
            mm = nc.tensor.matmul

            def repeated(ap, times):
                return bass.AP(ap.tensor, ap.offset, [list(ap.ap[0]), [0, times], list(ap.ap[-1])])

            pe.wait_ge(c_ident, 2)
            pe.wait_ge(in_w, 32)
            nc.tensor.transpose(psM[:, 0:D], w_sb[:, :], ident[:, :]).then_inc(c_pe, 1)
            pe.wait_ge(c_vec, 3)
            mm(psM[:, 0:D], wdT[:, :], wT[:, :], start=True, stop=True).then_inc(c_pe, 1)
            def recurrence(t):
                pe.wait_ge(rec_ev, t + 1)
                for c in range(t // 3 + 1):
                    k0, k1 = 3 * c, min(3 * c + 3, t + 1)
                    last = mm(R_BANKS[c][:, 0:(k1 - k0) * SLOT], Qm[:, :],
                              Rst[:, t % 2, 1 + k0:1 + k1, :], start=True, stop=True)
                last.then_inc(rec_mm, 1)

            def power(i, m):
                at = slice(m * P, (m + 1) * P)
                if m == 0:
                    pe.wait_ge(p_lo, NT)
                pe.wait_ge(pt_lo, NT * i if m == 0 else NT * (i - 1) + m + 1)
                for k in range(NT):
                    mm(P_BANKS[m][:, :], Ph[:, k, at], PTh[:, i - 1, k, :], start=k == 0, stop=False)
                    mm(P_BANKS[m][:, :], Ph[:, k, at], PTl[:, i - 1, k, :], start=False, stop=False)
                    last = mm(P_BANKS[m][:, :], Pl[:, k, at], PTh[:, i - 1, k, :],
                              start=False, stop=k == NT - 1)
                last.then_inc(pt_mm, 1)

            pe.wait_ge(in_fc, 32)
            pe.wait_ge(c_pool, 3)
            recurrence(0)
            for t in range(NT):
                pe.wait_ge(p_sb, t + 1)
                for m in range(NT):
                    last = nc.tensor.transpose(P_BANKS[m][:, t * P:(t + 1) * P],
                                               P_sb[:, t, m * P:(m + 1) * P], ident[:, :])
                    if t == NT - 1:
                        last.then_inc(pt_mm, 1)
            recurrence(1)
            for m in range(NT):
                power(1, m)
                recurrence(2 + m)
            power(2, 0)
            recurrence(6)
            power(2, 1)
            recurrence(7)
            power(2, 2)
            pe.wait_ge(bias_in, 2)
            for q in range(BLK):
                last = mm(psM[0:3 * QUAD, q * D:(q + 1) * D], bcols[:, q, :], ident[:, :], start=True, stop=True)
            last.then_inc(bias_mm, 1)
            for c in range(3):
                for q in range(4 * c, min(4 * c + 4, RS)):
                    last = nc.tensor.transpose(R_BANKS[c][:, (q - 4 * c) * D:(q - 4 * c + 1) * D],
                                               Rst[:, STEPS % 2, 1 + q, 0:D], ident[:, :])
                last.then_inc(rt_mm, 1)
            power(2, 3)
            pe.wait_ge(bias_lo, 1)
            pe.wait_ge(c_pool, 10)
            for i in range(PW):
                for k in range(NT if i else 1):
                    for part in (PTh, PTl) if i else (spread,):
                        last = mm(psM[0:3 * QUAD, :], sel[:, i, 0:3 * QUAD],
                                  part[:, i - 1, k, :] if i else repeated(part[:, :], N // D),
                                  start=i == 0, stop=i == PW - 1 and k == NT - 1 and part is PTl)
            last.then_inc(bias_mm, 1)
            pe.wait_ge(rt_ev, 3)

            def next_unit(g, index):
                if not isinstance(g, int) or g > 0 or index >= 2:
                    pe.wait_ge(l0_ev[index % 2], EPB * g + index // 2)

            def coefficients(bank_ap, block, n, alone):
                for t in range(TU):
                    nodes = slice((n * TU + t) * P, (n * TU + t + 1) * P)
                    mm(bank_ap[:, t * GD:(t + 1) * GD], Wst[0:3 * QUAD, nodes],
                       repeated(rb[0:3 * QUAD, block, :], GB), start=t == 0, stop=False)
                    for b in range(GB):
                        for i in range(PW):
                            last = mm(bank_ap[:, (t * GB + b) * D:(t * GB + b + 1) * D],
                                      zT[:, i, b, nodes], R[:, block * PW + i, :], start=False,
                                      stop=alone and t == TU - 1 and b == GB - 1 and i == PW - 1)
                return last

            def powers_of_x(g, n):
                index, power_, b = U_Z + n, n // GB, n % GB
                next_unit(g, index)
                if power_ == 0:
                    pe.wait_ge(x_split, g * GB + b + 1)
                for k in range(NT):
                    mm(psL[n % 2][:, :], Xh[:, b, k, :], PTh[:, power_, k, :], start=k == 0, stop=False)
                    mm(psL[n % 2][:, :], Xh[:, b, k, :], PTl[:, power_, k, :], start=False, stop=False)
                    last = mm(psL[n % 2][:, :], Xl[:, b, k, :], PTh[:, power_, k, :],
                              start=False, stop=k == NT - 1)
                last.then_inc(l0_mm, 1)

            def join(g, n):
                step, m = n // UPS, n % UPS
                if isinstance(g, int) and g == 0:
                    pe.wait_ge(pt_lo, PW * NT)
                for k in range(NT):
                    if m == 0 and k == TU:
                        pe.wait_ge(l0_ev[1], EPB * g + (U_B + n) // 2)
                    for t in range(TU):
                        nodes = slice((m * TU + t) * P, (m * TU + t + 1) * P)
                        out_ap = psL[n % 2][:, t * GD:(t + 1) * GD]
                        mm(out_ap, PTh[:, PW - 1, k, nodes], Yh[:, step, k, :], start=False, stop=False)
                        mm(out_ap, PTh[:, PW - 1, k, nodes], Yl[:, step, k, :], start=False, stop=False)
                        last = mm(out_ap, PTl[:, PW - 1, k, nodes], Yh[:, step, k, :],
                                  start=False, stop=(k == NT - 1 and t == TU - 1))
                last.then_inc(l0_mm, 1)

            def scores(a, h, i, fresh):
                s = s_unit(a, h, i)
                if i == 0:
                    pe.wait_ge(stacked[h], 6 * 16 * (a + 1))
                if not fresh or i >= 2:
                    pe.wait_ge(s_max, s - 1)
                mm(psS[i % 2][:, :], Qs[0:KS, h, i * P:(i + 1) * P], Ks[0:KS, h, :],
                   start=True, stop=True).then_inc(s_mm, 1)

            def iteration(g, j, horner, prep, attend, end):
                it = g * IPG + j
                a, p, e = it - ATT, it - PREP, it - END
                for kind, n, i in events(j, horner, prep, attend, end):
                    if kind in ("X1T", "Q", "K", "V"):
                        pe.wait_ge(m_ev, MPB * p + n)
                    if kind == "XT":
                        if n == 0:
                            pe.wait_ge(xin_in, 16 * (g + 1))
                        next_unit(g, U_X + n)
                        for t in range(NT):
                            last = nc.tensor.transpose(psL[n % 2][:, t * P:(t + 1) * P],
                                                       xin[:, n, t, :], ident[:, :])
                        last.then_inc(l0_mm, 1)
                    elif kind == "Z":
                        powers_of_x(g, n)
                    elif kind == "C":
                        next_unit(g, U_C + n)
                        pe.wait_ge(l0_ev[1], EPB * g + U_C // 2)
                        if isinstance(g, int) and g == 0:
                            pe.wait_ge(bias_lo, 2)
                        coefficients(psL[n % 2][:, :], BLK - 1, n, True).then_inc(l0_mm, 1)
                    elif kind == "BC":
                        next_unit(g, U_B + n)
                        coefficients(psL[n % 2][:, :], BLK - 2 - n // UPS, n % UPS, False)
                    elif kind == "BM":
                        join(g, n)
                    elif kind == "X1T":
                        pe.wait_ge(x1_done, p + 1)
                        for t in range(NT):
                            last = nc.tensor.transpose(psM[:, t * P:(t + 1) * P], x1[:, j, t, :], ident[:, :])
                        last.then_inc(m_mm, 1)
                    elif kind in ("Q", "K"):
                        cols = slice(0, D) if kind == "Q" else slice(D, 2 * D)
                        mm(psM[:, :], Wh[:, cols], x1Th[:, :], start=True, stop=False)
                        mm(psM[:, :], Wh[:, cols], x1Tl[:, :], start=False, stop=False)
                        mm(psM[:, :], Wl[:, cols], x1Th[:, :], start=False, stop=True).then_inc(m_mm, 1)
                    elif kind == "V":
                        cols = slice(2 * D, 3 * D)
                        for t in range(NT):
                            nodes = slice(t * P, (t + 1) * P)
                            mm(psM[:, nodes], x1Th[:, nodes], Wh[:, cols], start=True, stop=False)
                            mm(psM[:, nodes], x1Th[:, nodes], Wl[:, cols], start=False, stop=False)
                            last = mm(psM[:, nodes], x1Tl[:, nodes], Wh[:, cols], start=False, stop=True)
                        last.then_inc(m_mm, 1)
                    elif kind == "S":
                        scores(a, n, i, False)
                    elif kind == "S0":
                        scores(p, 0, i, not attend)
                    elif kind == "TR":
                        r = s_unit(a, n, i)
                        if i == 0:
                            pe.wait_ge(s_exp, s_unit(a, n, NT))
                        if horner or g == NG and j == 0 and n == 0 and i < 2:
                            pe.wait_ge(t_lo, r - 1 + T_FREE)
                        elif g == NG and j == 0 and n == 0:
                            pe.wait_ge(l0_ev[i % 2], EPB * NG)
                        else:
                            pe.wait_ge(t_lo, r - 3 + T_FREE)
                        for t in range(NT):
                            last = nc.tensor.transpose(e_bank(horner, i)[:, t * P:(t + 1) * P],
                                                       E[:, n % 2, t, i * P:(i + 1) * P], ident[:, :])
                        last.then_inc(t_mm, 1)
                    elif kind == "PV":
                        pe.wait_ge(t_lo, s_unit(a, n, NT) + T_FREE)
                        if n % 2 == 0:
                            pe.wait_ge(c_ev, a * 2 + n // 2 + C_FREE)
                        if n == 0:
                            pe.wait_ge(m_ev, MPB * (a + 1))
                        for t in range(NT):
                            for part in et(horner, n):
                                last = mm(psO[:, :], V[:, 1 - j, t, n // 2, n % 2, :], et_block(part, t),
                                          start=(n % 2 == 0 and t == 0 and part is et(horner, n)[0]),
                                          stop=(n % 2 == 1 and t == NT - 1 and part is et(horner, n)[1]))
                        if n % 2 == 1:
                            last.then_inc(o_mm, 1)
                    elif kind in ("CB", "CBF"):
                        pe.wait_ge(o_ev, (a if kind == "CB" else e) * 2 + n + 1)
                        for t in range(NT):
                            last = mm(psO[:, t * 2 * HD:(t + 1) * 2 * HD], oT[:, n, t * P:(t + 1) * P],
                                      fold[:, :], start=True, stop=True)
                        last.then_inc(c_mm, 1)

            run_iterations(pe, iteration)

        @block.vector
        def _(dve):
            V_ = nc.vector

            dve.wait_ge(in_w, 32)
            V_.tensor_scalar(dclip[:, :], dcol[:, :], 0.0, 1.0, ALU.max, ALU.min).then_inc(c_vec, 1)
            dve.wait_ge(c_pe, 1)
            dve.wait_ge(c_vec, 1)
            V_.tensor_copy(wT[:, :], psM[:, 0:D]).then_inc(c_vec, 1)
            V_.tensor_scalar(wdT[:, :], psM[:, 0:D], dclip[:, 0:1], None, ALU.mult).then_inc(c_vec, 1)
            dve.wait_ge(c_ident, 2)
            dve.wait_ge(c_pool, 3)
            for par in range(2):
                V_.tensor_scalar(Rst[:, par, 0, 0:D], ident[:, :], DT, None, ALU.mult)
            V_.tensor_scalar(decay_ident[:, :], ident[:, :], 1.0 - DT, None, ALU.mult).then_inc(c_vec, 1)
            dve.wait_ge(c_vec, 4)
            dve.wait_ge(c_pe, 2)
            V_.scalar_tensor_tensor(out=Qm[:, :], in0=psM[:, 0:D], scalar=DT, in1=decay_ident[:, :],
                                    op0=ALU.mult, op1=ALU.add).then_inc(rec_ev, 1)
            dve.wait_ge(c_act, 1)
            V_.tensor_scalar(nrate[:, :], rate[:, :], -DT / 4, -DT / 4, ALU.mult, ALU.add).then_inc(r_done, 1)
            dve.wait_ge(r_done, 1)
            V_.tensor_scalar(rate[:, :], nrate[:, :], -1.0, None, ALU.mult).then_inc(r_done, 1)
            dve.wait_ge(in_fc, 32)

            def recurrence(t):
                old, new = t % 2, (t + 1) % 2
                dve.wait_ge(rec_mm, t + 1)
                dve.wait_ge(rec_ev, t + 1)
                for c in range(t // 3 + 1):
                    k0, k1 = 3 * c, min(3 * c + 3, t + 1)
                    V_.tensor_tensor(Rst[:, new, 1 + k0:1 + k1, :],
                                     R_BANKS[c][:, 0:(k1 - k0) * SLOT].rearrange("p (k s) -> p k s", s=SLOT),
                                     Rst[:, old, k0:k1, :], ALU.add)
                V_.tensor_copy(Rst[:, new, 2 + t, :], Rst[:, old, 1 + t, :]).then_inc(rec_ev, 1)

            def power_low(i, m):
                dve.wait_ge(pt_hi, i * NT + m + 1)
                V_.tensor_tensor(PTl[:, i, m, :], P_BANKS[m][:, :], f(PTh[:, i, m, :]),
                                 ALU.subtract).then_inc(pt_lo, 1)

            recurrence(0)
            dve.wait_ge(in_adj, 16)
            dve.wait_ge(r_done, 2)
            for t in range(NT):
                V_.tensor_scalar(P_sb[:, t, :], adj_sb[:, t, :], rate[:, t:t + 1], None,
                                 ALU.mult).then_inc(r_done, 1)
                dve.wait_ge(r_done, 3 + t)
                diag = P_sb[:, t, t * P:(t + 1) * P]
                V_.scalar_tensor_tensor(out=diag, in0=ident[:, :], scalar=nrate[:, t:t + 1], in1=diag,
                                        op0=ALU.mult, op1=ALU.add).then_inc(p_sb, 1)
            for m in range(NT):
                power_low(0, m)
            recurrence(1)
            for m in range(NT):
                power_low(1, m)
                recurrence(2 + m)
            power_low(2, 0)
            recurrence(6)
            power_low(2, 1)
            recurrence(7)
            dve.wait_ge(c_pool, 4)
            dve.wait_ge(rec_ev, STEPS + 1)
            last_r = Rst[:, STEPS % 2]
            for h in range(3):
                k_cols = bass.AP(x1, bcols.offset + h * QUAD,
                                 [list(bcols.ap[0]), [3 * QUAD + PW, BLK], [1, PW]])
                ins = V_.tensor_copy(k_cols, last_r[:, 1:1 + RS, D].rearrange("p (q i) -> p q i", i=PW))
            ins.then_inc(bias_in, 1)
            V_.tensor_tensor(last_r[:, 1, 0:D], last_r[:, 1, 0:D], ident[:, :], ALU.add).then_inc(bias_in, 1)
            power_low(2, 2)
            dve.wait_ge(bias_hi, 1)
            V_.tensor_tensor(rb[2 * QUAD:3 * QUAD, :, :], psM[2 * QUAD:3 * QUAD, 0:BLK * D].rearrange(
                "p (q d) -> p q d", d=D), f(rb[2 * QUAD:3 * QUAD, :, :]), ALU.subtract).then_inc(bias_lo, 1)
            power_low(2, 3)
            dve.wait_ge(bias_hi, 2)
            V_.tensor_tensor(Wst[QUAD:2 * QUAD, :], psM[QUAD:2 * QUAD, :], f(Wst[QUAD:2 * QUAD, :]),
                             ALU.subtract).then_inc(bias_lo, 1)
            dve.wait_ge(c_act, 2)
            dve.wait_ge(c_pool, 15)
            V_.tensor_tensor(Wl[:, :], W_sb[:, :], f(Wh[:, :]), ALU.subtract).then_inc(c_vec, 1)
            V_.tensor_scalar(mask[:, :, :], adj_sb, 0.0, NEG, ALU.is_equal, ALU.mult).then_inc(c_vec, 1)
            dve.wait_ge(c_vec, 6)
            dve.wait_ge(rt_ev, 3)
            V_.memset(rec[:, :], 0.0).then_inc(t_lo, T_FREE)
            V_.memset(y[:, :, :], 0.0).then_inc(y_out, Y_FREE)
            V_.memset(negmax[:, :], 0.0).then_inc(c_ev, C_FREE)

            def low(bank_ap, hi, dst):
                return V_.tensor_tensor(dst, bank_ap, f(hi), ALU.subtract)

            def moments(which, count, src):
                s = ln[which]
                for t in range(NT):
                    ins = V_.bn_stats(stats[:, which, t, :], src(t))
                ins.then_inc(s, 1)
                dve.wait_ge(s, 3 * count + 1)
                carry_waits(dve, dve_passed)
                for t in range(NT):
                    ins = V_.bn_aggr(mv[:, which, t, :], stats[:, which, t, :])
                ins.then_inc(s, 1)
                dve.wait_ge(s, 3 * count + 2)
                V_.tensor_scalar(var[:, which, :], mv[:, which, :, 1], EPS, None, ALU.add).then_inc(s, 1)

            def normalise(which, count, src, dst):
                dve.wait_ge(root[which], count + 1)
                for t in range(NT):
                    ins = V_.tensor_scalar(dst(t), src(t), mv[:, which, t, 0:1],
                                           rstd[:, which, t:t + 1], ALU.subtract, ALU.mult)
                return ins

            def maximum(a, h, i, fresh):
                s = s_unit(a, h, i)
                at = h * NT + i
                dve.wait_ge(s_mm, s + 1)
                if not fresh or i >= 2:
                    dve.wait_ge(s_exp, s - 1)
                carry_waits(dve, dve_passed)
                V_.tensor_tensor_reduce(out=Sm[:, i % 2, :], in0=psS[i % 2][:, :], in1=mask[:, i, :],
                                        scale=-SCALE, scalar=3e38, op0=ALU.add, op1=ALU.min,
                                        accum_out=negmax[:, at:at + 1]).then_inc(s_max, 1)

            def iteration(g, j, horner, prep, attend, end):
                it = g * IPG + j
                a, p, e = it - ATT, it - PREP, it - END
                for kind, n, i in events(j, horner, prep, attend, end):
                    if kind == "C" or kind == "BM" and n < (BLK - 2) * UPS:
                        number = n if kind == "C" else UPS + n
                        dve.wait_ge(l0_hi, (BLK - 1) * UPS * g + number + 1)
                        low(psL[n % 2][:, :], Yh[:, number // UPS, units(n), :],
                            Yl[:, number // UPS, units(n), :]).then_inc(l0_ev[n % 2], 1)
                    elif kind == "LN1A":
                        for bank_ev in l0_ev:
                            dve.wait_ge(bank_ev, EPB * g)
                        moments(0, p, lambda t: u[:, t, j * D:(j + 1) * D])
                    elif kind == "LN1B":
                        normalise(0, p, lambda t: u[:, t, j * D:(j + 1) * D],
                                  lambda t: x1[:, j, t, :]).then_inc(x1_done, 1)
                    elif kind in ("X1L", "QL", "KL", "VL"):
                        dve.wait_ge(m_hi, MPB * p + n + 1)
                        if kind == "VL":
                            for e_ in range(2):
                                ins = low(v_part(psM, e_), V[:, j, :, :, e_, 2 * HD * e_:2 * HD * e_ + HD],
                                          V[:, j, :, :, e_, 2 * HD * e_ + HD:2 * HD * (e_ + 1)])
                            ins.then_inc(m_ev, 1)
                        else:
                            h_, l_ = {"X1L": (x1Th, x1Tl), "QL": (qh, ql), "KL": (kh, kl)}[kind]
                            low(psM[:, :], h_[:, :], l_[:, :]).then_inc(m_ev, 1)
                    elif kind == "S":
                        maximum(a, n, i, False)
                    elif kind == "S0":
                        maximum(p, 0, i, not attend)
                    elif kind == "TR":
                        dve.wait_ge(t_hi, s_unit(a, n, i) + 1)
                        low(e_bank(horner, i)[:, :], *(et_block(part, i) for part in et(horner, n))).then_inc(t_lo, 1)
                    elif kind in ("CB", "CBF"):
                        done = (a if kind == "CB" else e) * 2 + n + 1
                        dve.wait_ge(c_mm, done)
                        V_.reciprocal(rec[:, :], sums[:, n * 2 * NT:(n + 1) * 2 * NT]).then_inc(r_done, 1)
                        dve.wait_ge(r_done, 6 + done)
                        r_b = bass.AP(rec, 0, [list(rec[:, :].ap[0]), [1, NT], [NT, 2], [0, HD]])
                        V_.tensor_tensor(
                            att[:, :, n * 2 * HD:(n + 1) * 2 * HD].rearrange("p t (e d) -> p t e d", e=2),
                            psO[:, 0:NT * 2 * HD].rearrange("p (t e d) -> p t e d", e=2, d=HD), r_b,
                            ALU.mult).then_inc(c_ev, 1)
                    elif kind == "LN2A":
                        dve.wait_ge(c_ev, e * 2 + 2 + C_FREE)
                        V_.tensor_tensor(att[:, :, :], att[:, :, :], x1[:, j, :, :], ALU.add).then_inc(z_done, 1)
                        dve.wait_ge(z_done, e + 1)
                        moments(1, e, lambda t: att[:, t, :])
                    elif kind == "LN2B":
                        dve.wait_ge(y_out, 16 * e + Y_FREE)
                        normalise(1, e, lambda t: att[:, t, :], lambda t: y[:, t, :]).then_inc(y_done, 1)

            run_iterations(dve, iteration)


_INS = ["x", "adj", "L0_gnn_alpha_train", "L0_gnn_w", "L0_gnn_d", "L0_gnn_fc_in_w", "L0_gnn_fc_in_b", "L1_gnn_W"]


def kernel(**inputs):
    import numpy as _np
    import concourse.bacc as _bacc
    from concourse import mybir as _mybir
    from concourse.bass_utils import run_bass_kernel_spmd as _run

    nc = _bacc.Bacc("TRN2", target_bir_lowering=False, num_devices=1)
    arrays, args = {}, []
    for name in _INS:
        a = _np.ascontiguousarray(inputs[name])
        arrays[f"in_{name}_dram"] = a
        args.append(nc.dram_tensor(f"in_{name}_dram", a.shape, _mybir.dt.from_np(a.dtype), kind="ExternalInput").ap())
    args.append(nc.dram_tensor("out_0_dram", (B, N, D), _mybir.dt.float32, kind="ExternalOutput").ap())
    gnn_kernel(nc, *args)
    r = _run(nc, [arrays], core_ids=[0])
    return r.results[0]["out_0_dram"]
```

```python
from contextlib import ExitStack

import concourse.bass as bass
from concourse import mybir

F32 = mybir.dt.float32
F32R = mybir.dt.float32r
ALU = mybir.AluOpType
ACT = mybir.ActivationFunctionType

B, N, D = 16, 512, 128
P = 128
NT = N // P
GB = 2
GD = GB * D
TU = N // GD
UPS = NT // TU
NG = B // GB
STEPS = 8
DT = 1.0 / STEPS
H = 4
HD = D // H
SCALE = HD ** -0.5
EPS = 1e-5
NEG = -1e30
SLOT = D + 2
RS = STEPS + 1
PW = 3
BLK = RS // PW
QUAD = 32
VW = 6 * HD
KS = 3 * HD

IPG = GB
PREP = IPG
ATT = IPG + 1
END = IPG + 2
U_X, U_Z, U_C = 0, GB, PW * GB
U_B = U_C + UPS
UPG = U_B + (BLK - 1) * UPS
EPB = UPG // 2

EVENTS = [
    ("HORNER", 0, 0), ("TR", 0, 0), ("TR", 0, 1), ("S", 1, 0), ("S", 1, 1), ("LN1A", 0, 0),
    ("HORNER", 1, 0),
    ("TR", 0, 2), ("TR", 0, 3), ("S", 1, 2), ("S", 1, 3), ("LN1B", 0, 0),
    ("HORNER", 2, 0), ("PVF", 3, 0),
    ("TR", 1, 0), ("TR", 1, 1), ("S", 2, 0), ("S", 2, 1), ("CBF", 1, 0),
    ("HORNER", 3, 0), ("X1T", 0, 0),
    ("TR", 1, 2), ("TR", 1, 3), ("S", 2, 2), ("S", 2, 3), ("LN2A", 0, 0),
    ("HORNER", 4, 0), ("Q", 1, 0), ("QL", 1, 0), ("PV", 0, 0),
    ("TR", 2, 0), ("TR", 2, 1), ("S", 3, 0), ("S", 3, 1), ("LN2B", 0, 0),
    ("HORNER", 5, 0), ("K", 2, 0), ("KL", 2, 0),
    ("TR", 2, 2), ("TR", 2, 3), ("S", 3, 2), ("S", 3, 3),
    ("HORNER", 6, 0), ("PV", 1, 0),
    ("TR", 3, 0), ("TR", 3, 1), ("S0", 0, 0), ("S0", 0, 1), ("CB", 0, 0),
    ("HORNER", 7, 0), ("V", 3, 0),
    ("TR", 3, 2), ("TR", 3, 3), ("S0", 0, 2), ("S0", 0, 3), ("VL", 3, 0),
    ("HORNER", 8, 0), ("PV", 2, 0),
]
LATE_EVENTS = [
    ("S", 1, 0), ("S", 1, 1), ("LN1A", 0, 0), ("S", 1, 2), ("S", 1, 3),
    ("TR", 0, 0), ("TR", 0, 1), ("TR", 0, 2), ("TR", 0, 3),
    ("S", 2, 0), ("S", 2, 1), ("PVF", 3, 0), ("LN1B", 0, 0), ("S", 2, 2), ("S", 2, 3), ("CBF", 1, 0),
    ("X1T", 0, 0),
    ("TR", 1, 0), ("TR", 1, 1), ("TR", 1, 2), ("TR", 1, 3),
    ("Q", 1, 0), ("S", 3, 0), ("S", 3, 1), ("PV", 0, 0), ("S", 3, 2), ("QL", 1, 0), ("S", 3, 3), ("K", 2, 0),
    ("LN2A", 0, 0), ("KL", 2, 0),
    ("TR", 2, 0), ("TR", 2, 1), ("TR", 2, 2), ("TR", 2, 3), ("PV", 1, 0), ("LN2B", 0, 0),
    ("TR", 3, 0), ("TR", 3, 1), ("CB", 0, 0), ("TR", 3, 2), ("TR", 3, 3), ("V", 3, 0), ("VL", 3, 0),
    ("S0", 0, 0), ("S0", 0, 1), ("PV", 2, 0), ("S0", 0, 2), ("S0", 0, 3),
    ("S0", 1, 0), ("S0", 1, 1), ("S0", 1, 2), ("S0", 1, 3),
]
HORNER = [
    [[("XT", 0)], [("XT", 1), ("Z", 0)], [("Z", 1)], [("Z", 2)], [("Z", 3)],
     [("C", 0)], [("C", 1)], [], [("BC", 0)]],
    [[], [("BM", 0)], [("BC", 1)], [("BM", 1)], [("BC", 2), ("XS", 0), ("XS", 1)], [("BM", 2)],
     [("BC", 3)], [], [("BM", 3)]],
]
PREP_KINDS = ("LN1A", "LN1B", "X1T", "Q", "QL", "K", "KL", "V", "VL", "S0")
ATT_KINDS = ("TR", "S", "PV", "CB")
END_KINDS = ("PVF", "CBF", "LN2A", "LN2B")
MPB = 4


def events(j, horner, prep, att, end):
    late = att and not horner
    for kind, n, i in LATE_EVENTS if late else EVENTS:
        if late and kind == "S" and n == 1 and not (prep and j == 0):
            continue
        if kind == "HORNER":
            for piece, m in HORNER[j][n] if horner else ():
                yield piece, m, 0
        elif prep and kind in PREP_KINDS or att and kind in ATT_KINDS or end and kind in END_KINDS:
            yield kind, n, i


def run_iterations(eng, iteration):
    for j in range(IPG):
        iteration(0, j, True, False, False, False)
    for j in range(IPG):
        iteration(1, j, True, True, j > 0, False)
    with eng.Fori(2, NG - 1) as g:
        for j in range(IPG):
            iteration(g, j, True, True, True, True)
    for j in range(IPG):
        iteration(NG - 1, j, True, True, True, True)
    for j in range(IPG):
        iteration(NG, j, False, True, True, True)
    iteration(NG + 1, 0, False, False, True, True)
    iteration(NG + 1, 1, False, False, False, True)


def carry_waits(eng, passed):
    eng.sem_inc(passed, 1)


def gnn_kernel(nc, x, adj, alpha, w, d, fc_w, fc_b, w_qkv, out):
    with ExitStack() as ctx:
        def sb(name, shape, dt=F32):
            return ctx.enter_context(nc.sbuf_tensor(name, shape, dt))

        def sem(name):
            return ctx.enter_context(nc.semaphore(name))

        ident = sb("ident", [P, P])
        mask = sb("mask", [P, NT, N])
        PTh = sb("PTh", [P, PW, NT, N], F32R)
        PTl = sb("PTl", [P, PW, NT, N], F32R)
        R = sb("R", [P, RS, D])
        rb = sb("rb", [P, BLK, D], F32R)
        Wst = sb("Wst", [P, N], F32R)
        W_sb = sb("W_sb", [P, 3 * D])
        dcol = sb("dcol", [P, 1])
        dclip = sb("dclip", [P, 1])
        alph = sb("alph", [P, NT])
        rate = sb("rate", [P, NT])
        nrate = sb("nrate", [P, NT])
        xin = sb("xin", [P, GB, NT, D])
        zT = sb("zT", [P, PW, GB, N])
        Yh = sb("Yh", [P, 2, NT, GD], F32R)
        Yl = sb("Yl", [P, 2, NT, GD], F32R)
        Xh, Xl = (bass.AP(part, 0, [[2 * NT * GD, P], [NT * D, GB], [D, NT], [1, D]]) for part in (Yh, Yl))
        u = sb("u", [P, NT, GD])
        x1 = sb("x1", [P, NT, D])
        x1res = sb("x1res", [P, 2, NT, D])
        x1T = sb("x1T", [P, N])
        qh = sb("qh", [P, N], F32R)
        ql = sb("ql", [P, N], F32R)
        kh = sb("kh", [P, N], F32R)
        kl = sb("kl", [P, N], F32R)
        Qs = sb("Qs", [P, H, N], F32R)
        Ks = sb("Ks", [P, H, N], F32R)
        sel = Ks[:, 0:PW, 0:P]
        spread = Ks[:, PW, 0:D]
        V = sb("V", [P, 2, NT, H // 2, VW], F32R)
        w_sb, wT, wdT, Qm = (x1res[:, 0, t, :] for t in range(4))
        decay_ident = x1res[:, 1, 3, :]
        bcols = bass.AP(x1res, NT * D, [list(x1res[:, 0, 0, :].ap[0]), [3 * QUAD, BLK], [1, 3 * QUAD]])
        Sm = sb("Sm", [P, 2, N])
        negmax = sb("negmax", [P, H * NT])
        E = sb("E", [P, 2, NT, N])
        ETh = sb("ETh", [P, 2, NT, N], F32R)
        ETl = sb("ETl", [P, 2, NT, N], F32R)
        oT = sb("oT", [P, N])
        sums = sb("sums", [P, 2, H * NT])
        rec = sb("rec", [P, 2 * NT])
        o_sum = sb("o_sum", [P, NT, 2, HD])
        att = sb("att", [P, NT, D])
        y = sb("y", [P, NT, D])
        stats = sb("stats", [P, 2, NT, 6])
        mv = sb("mv", [P, 2, NT, 2])
        var = sb("var", [P, 2, NT])
        rstd = sb("rstd", [P, 2, NT])
        minus_half = sb("minus_half", [P, NT])
        Rst = bass.AP(zT, 0, [list(zT[:, 0, 0, :].ap[0]), [(RS + 1) * SLOT, 2], [SLOT, RS + 1], [1, SLOT]])
        P_sb = E[:, 0, :, :]
        adj_sb = E[:, 1, :, :]
        Ph, Pl = ETh[:, 0], ETl[:, 0]

        def bank(name):
            return ctx.enter_context(nc.psum_tensor(name, [P, N], F32))

        psL = [bank("psL0"), bank("psL1")]
        psS = [bank("psS0"), bank("psS1")]
        psE = [bank("psE0"), bank("psE1")]
        psO = bank("psO")
        psM = bank("psM")
        R_BANKS = [psL[0], psL[1], psO]
        P_BANKS = psS + psE

        in_w = sem("in_w")
        in_adj = [sem(f"in_adj{t}") for t in range(NT)]
        in_fc = sem("in_fc")
        in_qkv = sem("in_qkv")
        in_alpha = sem("in_alpha")
        c_ident = sem("c_ident")
        c_pool = sem("c_pool")
        dve_passed = sem("dve_passed")
        pool_passed = sem("pool_passed")
        c_pow = sem("c_pow")
        c_vec = sem("c_vec")
        c_act = sem("c_act")
        c_pe = sem("c_pe")
        rec_mm = sem("rec_mm")
        rec_ev = sem("rec_ev")
        p_sb = sem("p_sb")
        p_hi = sem("p_hi")
        p_lo = sem("p_lo")
        pt_mm = sem("pt_mm")
        pt_hi = sem("pt_hi")
        pt_lo = sem("pt_lo")
        rt_mm = sem("rt_mm")
        rt_ev = sem("rt_ev")
        bias_in = sem("bias_in")
        bias_mm = sem("bias_mm")
        bias_hi = sem("bias_hi")
        bias_lo = sem("bias_lo")
        xin_in = sem("xin_in")
        l0_mm = sem("l0_mm")
        l0_hi = sem("l0_hi")
        l0_ev = [sem("l0_ev0"), sem("l0_ev1")]
        x_high = sem("x_high")
        x_split = sem("x_split")
        x1_done = sem("x1_done")
        x1_kept = sem("x1_kept")
        m_mm = sem("m_mm")
        m_hi = sem("m_hi")
        m_ev = sem("m_ev")
        stacked = [sem(f"stacked{h}") for h in range(H)]
        s_mm = sem("s_mm")
        s_max = sem("s_max")
        s_exp = sem("s_exp")
        t_mm = sem("t_mm")
        t_hi = sem("t_hi")
        t_lo = sem("t_lo")
        o_mm = sem("o_mm")
        o_ev = sem("o_ev")
        c_mm = sem("c_mm")
        c_ev = sem("c_ev")
        r_done = sem("r_done")
        att_done = sem("att_done")
        z_done = sem("z_done")
        y_done = sem("y_done")
        y_out = sem("y_out")
        ln = [sem("ln1"), sem("ln2")]
        root = [sem("root1"), sem("root2")]
        T_FREE = 2
        C_FREE = 1
        Y_FREE = 16

        def f(ap):
            return ap.bitcast(F32)

        def e_bank(horner, i):
            return psE[i % 2] if horner else (psE + psL)[i]

        def is_last(g):
            return isinstance(g, int) and g == NG - 1

        def units(n):
            return slice(n * TU, (n + 1) * TU)

        def v_part(bank_ap, e):
            return bank_ap[:, :].rearrange("p (t b e d) -> p t b e d", b=H // 2, e=2, d=HD)[:, :, :, e, :]

        def s_unit(a, h, i):
            return (a * H + h) * NT + i

        x_v = x.rearrange("b (t p) d -> p b t d", p=P)
        out_v = out.rearrange("b (t p) d -> p b t d", p=P)

        block = ctx.enter_context(nc.Block())

        @block.sync
        def _(sp):
            sp.dma_start(w_sb[:, :], w).then_inc(in_w, 16)
            sp.dma_start(dcol[:, :], d.rearrange("(p a) -> p a", a=1)).then_inc(in_w, 16)
            sp.dma_start(alph[:, :], alpha.rearrange("(t p) -> p t", p=P),
                         allow_slow_non_contiguous=True).then_inc(in_alpha, 16)
            for t in range(NT):
                sp.dma_start(adj_sb[:, t, :], adj[t * P:(t + 1) * P, :]).then_inc(in_adj[t], 16)
            sp.dma_start(Rst[:, 0, 1, 0:D], fc_w).then_inc(in_fc, 16)
            sp.dma_start(Rst[:, 0, 1, D:D + 1], fc_b.rearrange("(p a) -> p a", a=1)).then_inc(in_fc, 16)
            sp.dma_start(W_sb[:, :], w_qkv).then_inc(in_qkv, 16)
            sp.dma_start(xin[:, :, :, :], x_v[:, 0:GB]).then_inc(xin_in, 16)

            def iteration(g, j, horner, prep, attend, end):
                it = g * IPG + j
                if horner and j == 0 and not is_last(g):
                    sp.wait_ge(l0_mm, UPG * g + GB)
                    sp.wait_ge(x_split, (g + 1) * GB)
                    sp.dma_start(xin[:, :, :, :], x_v[:, bass.ds((g + 1) * GB, GB)]).then_inc(xin_in, 16)

                def store():
                    sp.wait_ge(y_done, it - END + 1)
                    sp.dma_start(out_v[:, bass.ds(it - END, 1)],
                                 y[:, :, :].rearrange("p (o t) d -> p o t d", o=1)).then_inc(y_out, 16)

                def stack(dst, parts, h):
                    rows = slice(h * HD, (h + 1) * HD)
                    for r, part in enumerate(parts):
                        sp.dma_start(f(dst[r * HD:(r + 1) * HD, h, :]),
                                     f(part[rows, :])).then_inc(stacked[h], 16)

                if end and (horner or not prep):
                    store()
                if prep:
                    for h in range(H):
                        if attend:
                            sp.wait_ge(s_mm, s_unit(it - ATT, h, NT))
                        if h == 0:
                            sp.wait_ge(m_ev, MPB * (it - PREP) + 2)
                        stack(Qs, (qh, ql, qh), h)
                        if h == 0:
                            sp.wait_ge(m_ev, MPB * (it - PREP) + 3)
                        stack(Ks, (kh, kh, kl), h)
                        if not horner and h == 1:
                            store()

            run_iterations(sp, iteration)
            sp.wait_ge(y_out, 16 * B + Y_FREE)

        @block.gpsimd
        def _(pool):
            nc.gpsimd.memset(ident[:, :], 0.0).then_inc(c_ident, 1)
            pool.wait_ge(c_ident, 1)
            nc.gpsimd.affine_select(out=ident[:, :], in_=ident[:, :], compare_op=ALU.not_equal, fill=1.0,
                                    base=0, pattern=[[-1, P]], channel_multiplier=1).then_inc(c_ident, 1)
            nc.gpsimd.memset(Rst[:, 1, 1:RS + 1, :], 0.0).then_inc(c_pool, 1)
            nc.gpsimd.memset(Rst[:, 0, 2:RS + 1, :], 0.0)
            nc.gpsimd.memset(Rst[:, 0, 1, D + 1:SLOT], 0.0).then_inc(c_pool, 1)
            nc.gpsimd.memset(Rst[:, :, 0, :], 0.0).then_inc(c_pool, 1)
            nc.gpsimd.memset(bcols[:, :, :], 0.0).then_inc(c_pool, 1)
            nc.gpsimd.memset(f(sel[:, :, :]), 0.0).then_inc(c_pool, 1)
            nc.gpsimd.memset(f(spread[:, :]), 1.0 / P).then_inc(c_pool, 1)
            nc.gpsimd.memset(minus_half[:, :], -0.5).then_inc(c_pow, 1)
            pool.wait_ge(c_pow, 1)
            pool.wait_ge(c_pool, 6)
            for i in range(PW):
                nc.gpsimd.memset(f(sel[:, i, :]).rearrange("p (h r) -> p h r", r=QUAD)[:, 0:3, i:RS:PW],
                                 1.0).then_inc(c_pool, 1)
            for t in range(NT):
                pool.wait_ge(p_hi, t + 1)
                nc.gpsimd.tensor_tensor(Pl[:, t, :], P_sb[:, t, :], f(Ph[:, t, :]),
                                        ALU.subtract).then_inc(p_lo, 1)
            nc.gpsimd.memset(f(V[:, :, :, :, :]), 0.0).then_inc(c_pool, 1)

            def low_x(g, b):
                pool.wait_ge(x_high, g * GB + b + 1)
                nc.gpsimd.tensor_tensor(Xl[:, b], xin[:, b], f(Xh[:, b]), ALU.subtract).then_inc(x_split, 1)

            for b in range(GB):
                low_x(0, b)

            def inverse_root(which, count):
                pool.wait_ge(ln[which], 3 * count + 3)
                nc.gpsimd.tensor_tensor(rstd[:, which, :], var[:, which, :], minus_half[:, :],
                                        ALU.pow).then_inc(root[which], 1)

            def iteration(g, j, horner, prep, attend, end):
                it = g * IPG + j
                if prep:
                    inverse_root(0, it - PREP)
                if end:
                    inverse_root(1, it - END)
                if prep:
                    pool.wait_ge(x1_done, it - PREP + 1)
                    if end:
                        pool.wait_ge(z_done, it - END + 1)
                    carry_waits(pool, pool_passed)
                    nc.gpsimd.tensor_copy(x1res[:, j, :, :], x1[:, :, :]).then_inc(x1_kept, 1)
                if horner and j == 1 and not is_last(g):
                    for b in range(GB):
                        low_x(g + 1, b)

            run_iterations(pool, iteration)

        @block.scalar
        def _(act):
            act.wait_ge(in_alpha, 16)
            nc.scalar.activation(rate[:, :], alph[:, :], ACT.Tanh, scale=0.5).then_inc(c_act, 1)
            for t in range(NT):
                act.wait_ge(p_sb, t + 1)
                nc.scalar.activation(Ph[:, t, :], P_sb[:, t, :], ACT.Copy).then_inc(p_hi, 1)

            def power_high(i, m):
                act.wait_ge(pt_mm, i * NT + m + 1)
                nc.scalar.activation(PTh[:, i, m, :], P_BANKS[m][:, :], ACT.Copy).then_inc(pt_hi, 1)

            for i in range(PW - 1):
                for m in range(NT):
                    power_high(i, m)

            def split_x(g, b):
                if b == 0:
                    act.wait_ge(xin_in, 16 * (g + 1))
                nc.scalar.activation(Xh[:, b], xin[:, b], ACT.Copy).then_inc(x_high, 1)

            power_high(2, 0)
            for b in range(GB):
                split_x(0, b)
            power_high(2, 1)
            power_high(2, 2)
            power_high(2, 3)
            act.wait_ge(bias_mm, 1)
            nc.scalar.activation(Wst[0:3 * QUAD, :], psM[0:3 * QUAD, :], ACT.Copy).then_inc(bias_hi, 1)
            for c in range(3):
                q0, q1 = 4 * c, min(4 * c + 4, RS)
                act.wait_ge(rt_mm, c + 1)
                nc.scalar.activation(R[:, q0:q1, :], R_BANKS[c][:, 0:(q1 - q0) * D].rearrange(
                    "p (q d) -> p q d", d=D), ACT.Copy).then_inc(rt_ev, 1)
            act.wait_ge(bias_mm, 2)
            nc.scalar.activation(rb[0:3 * QUAD, :, :], psM[0:3 * QUAD, 0:BLK * D].rearrange(
                "p (q d) -> p q d", d=D), ACT.Copy).then_inc(bias_hi, 1)

            def high(bank_ap, dst):
                return nc.scalar.activation(dst, bank_ap, ACT.Copy)

            def exponential(a, parity, h, i, fresh):
                s = s_unit(a, h, i)
                act.wait_ge(s_max, s + 1)
                if not fresh:
                    act.wait_ge(t_lo, s_unit(a, h - 1, 0) + T_FREE)
                nc.scalar.activation(E[:, h % 2, i, :], Sm[:, i % 2, :], ACT.Exp, scale=-1.0,
                                     bias=negmax[:, h * NT + i:h * NT + i + 1],
                                     accum_out=sums[:, parity, h * NT + i:h * NT + i + 1]).then_inc(s_exp, 1)

            def iteration(g, j, horner, prep, attend, end):
                it = g * IPG + j
                a, p, e = it - ATT, it - PREP, it - END
                for kind, n, i in events(j, horner, prep, attend, end):
                    if kind == "XS":
                        if not is_last(g):
                            split_x(g + 1, n)
                    elif kind in ("XT", "Z"):
                        act.wait_ge(l0_mm, UPG * g + (U_Z if kind == "Z" else U_X) + n + 1)
                        power = 0 if kind == "XT" else n // GB + 1
                        nc.scalar.activation(zT[:, power, n % GB, :], psL[n % 2][:, :],
                                             ACT.Copy).then_inc(l0_ev[n % 2], 1)
                    elif kind == "C":
                        act.wait_ge(l0_mm, UPG * g + U_C + n + 1)
                        high(psL[n % 2][:, :], Yh[:, 0, units(n), :]).then_inc(l0_hi, 1)
                    elif kind == "BM":
                        act.wait_ge(l0_mm, UPG * g + U_B + n + 1)
                        if n < (BLK - 2) * UPS:
                            high(psL[n % 2][:, :], Yh[:, 1, units(n), :]).then_inc(l0_hi, 1)
                        else:
                            if not isinstance(g, int) or g > 0:
                                act.wait_ge(x1_done, g * GB)
                            nc.scalar.activation(u[:, units(n % UPS), :], psL[n % 2][:, :],
                                                 ACT.Copy).then_inc(l0_ev[n % 2], 1)
                    elif kind == "X1T":
                        act.wait_ge(m_mm, MPB * p + 1)
                        nc.scalar.activation(x1T[:, :], psM[:, :], ACT.Copy).then_inc(m_ev, 1)
                    elif kind in ("Q", "K", "VL"):
                        act.wait_ge(m_mm, MPB * p + n + 1)
                        if kind == "VL":
                            for e_ in range(2):
                                ins = high(v_part(psM, e_), V[:, j, :, :, 4 * HD * e_:4 * HD * e_ + HD])
                            ins.then_inc(m_hi, 1)
                            continue
                        if kind == "Q":
                            for h in range(H):
                                act.wait_ge(stacked[h], 6 * 16 * p)
                        dst = {"Q": qh, "K": kh}[kind]
                        high(psM[:, :], dst[:, :]).then_inc(m_hi, 1)
                    elif kind == "S":
                        exponential(a, 1 - j, n, i, False)
                    elif kind == "S0":
                        exponential(p, j, n, i, not attend)
                    elif kind == "TR":
                        act.wait_ge(t_mm, s_unit(a, n, i) + 1)
                        high(e_bank(horner, i)[:, :], ETh[:, n % 2, i, :]).then_inc(t_hi, 1)
                    elif kind in ("PV", "PVF") and n % 2 == 1:
                        act.wait_ge(o_mm, (a if kind == "PV" else e) * 2 + n // 2 + 1)
                        nc.scalar.activation(oT[:, :], psO[:, :], ACT.Copy).then_inc(o_ev, 1)

            run_iterations(act, iteration)

        @block.tensor
        def _(pe):
            mm = nc.tensor.matmul

            def repeated(ap, times):
                return bass.AP(ap.tensor, ap.offset, [list(ap.ap[0]), [0, times], list(ap.ap[-1])])

            pe.wait_ge(c_ident, 2)
            pe.wait_ge(in_w, 32)
            nc.tensor.transpose(psM[:, 0:D], w_sb[:, :], ident[:, :]).then_inc(c_pe, 1)
            pe.wait_ge(c_vec, 3)
            mm(psM[:, 0:D], wdT[:, :], wT[:, :], start=True, stop=True).then_inc(c_pe, 1)

            def recurrence(t):
                pe.wait_ge(rec_ev, t + 1)
                for c in range(t // 3 + 1):
                    k0, k1 = 3 * c, min(3 * c + 3, t + 1)
                    last = mm(R_BANKS[c][:, 0:(k1 - k0) * SLOT], Qm[:, :],
                              Rst[:, t % 2, 1 + k0:1 + k1, :], start=True, stop=True)
                last.then_inc(rec_mm, 1)

            def power(i, m):
                at = slice(m * P, (m + 1) * P)
                if m == 0:
                    pe.wait_ge(p_hi, NT)
                    pe.wait_ge(pt_hi, NT * i)
                pe.wait_ge(pt_lo, NT * (i - 1) + m + 1)
                for left, right, ready, count in ((Ph, PTh, None, 0), (Ph, PTl, pt_lo, NT * i),
                                                  (Pl, PTh, p_lo, NT)):
                    if m == 0 and ready is not None:
                        pe.wait_ge(ready, count)
                    for k in range(NT):
                        last = mm(P_BANKS[m][:, :], left[:, k, at], right[:, i - 1, k, :],
                                  start=left is Ph and right is PTh and k == 0, stop=left is Pl and k == NT - 1)
                last.then_inc(pt_mm, 1)

            for t in range(NT):
                pe.wait_ge(p_sb, t + 1)
                for m in range(NT):
                    last = nc.tensor.transpose(P_BANKS[m][:, t * P:(t + 1) * P],
                                               P_sb[:, t, m * P:(m + 1) * P], ident[:, :])
                    if t == NT - 1:
                        last.then_inc(pt_mm, 1)
            pe.wait_ge(in_fc, 32)
            pe.wait_ge(c_pool, 3)
            recurrence(0)
            for m in range(NT):
                power(1, m)
                recurrence(1 + m)
            for m in range(NT - 1):
                power(2, m)
                recurrence(5 + m)
            power(2, NT - 1)
            pe.wait_ge(c_pool, 9)
            for i in range(PW):
                for k in range(NT if i else 1):
                    for part in (PTh, PTl) if i else (spread,):
                        last = mm(psM[0:3 * QUAD, :], sel[:, i, 0:3 * QUAD],
                                  part[:, i - 1, k, :] if i else repeated(part[:, :], N // D),
                                  start=i == 0, stop=i == PW - 1 and k == NT - 1 and part is PTl)
            last.then_inc(bias_mm, 1)
            pe.wait_ge(bias_in, 2)
            for c in range(3):
                for q in range(4 * c, min(4 * c + 4, RS)):
                    last = nc.tensor.transpose(R_BANKS[c][:, (q - 4 * c) * D:(q - 4 * c + 1) * D],
                                               Rst[:, STEPS % 2, 1 + q, 0:D], ident[:, :])
                last.then_inc(rt_mm, 1)
            pe.wait_ge(bias_lo, 1)
            for q in range(BLK):
                last = mm(psM[0:3 * QUAD, q * D:(q + 1) * D], bcols[:, q, :], ident[:, :], start=True, stop=True)
            last.then_inc(bias_mm, 1)
            pe.wait_ge(in_qkv, 16)
            pe.wait_ge(rt_ev, 3)

            def next_unit(g, index):
                if not isinstance(g, int) or g > 0 or index >= 2:
                    pe.wait_ge(l0_ev[index % 2], EPB * g + index // 2)

            def coefficients(bank_ap, block, n, alone):
                for t in range(TU):
                    nodes = slice((n * TU + t) * P, (n * TU + t + 1) * P)
                    mm(bank_ap[:, t * GD:(t + 1) * GD], Wst[0:3 * QUAD, nodes],
                       repeated(rb[0:3 * QUAD, block, :], GB), start=t == 0, stop=False)
                    for b in range(GB):
                        for i in range(PW):
                            last = mm(bank_ap[:, (t * GB + b) * D:(t * GB + b + 1) * D],
                                      zT[:, i, b, nodes], R[:, block * PW + i, :], start=False,
                                      stop=alone and t == TU - 1 and b == GB - 1 and i == PW - 1)
                return last

            def powers_of_x(g, n):
                index, power_, b = U_Z + n, n // GB, n % GB
                next_unit(g, index)
                if power_ == 0:
                    pe.wait_ge(x_split, g * GB + b + 1)
                for k in range(NT):
                    mm(psL[n % 2][:, :], Xh[:, b, k, :], PTh[:, power_, k, :], start=k == 0, stop=False)
                    mm(psL[n % 2][:, :], Xh[:, b, k, :], PTl[:, power_, k, :], start=False, stop=False)
                    last = mm(psL[n % 2][:, :], Xl[:, b, k, :], PTh[:, power_, k, :],
                              start=False, stop=k == NT - 1)
                last.then_inc(l0_mm, 1)

            def join(g, n):
                step, m = n // UPS, n % UPS
                if isinstance(g, int) and g == 0:
                    pe.wait_ge(pt_lo, PW * NT)
                for k in range(NT):
                    if m == 0 and k == TU:
                        pe.wait_ge(l0_ev[1], EPB * g + (U_B + n) // 2)
                    for t in range(TU):
                        nodes = slice((m * TU + t) * P, (m * TU + t + 1) * P)
                        out_ap = psL[n % 2][:, t * GD:(t + 1) * GD]
                        mm(out_ap, PTh[:, PW - 1, k, nodes], Yh[:, step, k, :], start=False, stop=False)
                        mm(out_ap, PTh[:, PW - 1, k, nodes], Yl[:, step, k, :], start=False, stop=False)
                        last = mm(out_ap, PTl[:, PW - 1, k, nodes], Yh[:, step, k, :],
                                  start=False, stop=(k == NT - 1 and t == TU - 1))
                last.then_inc(l0_mm, 1)

            def scores(a, h, i, fresh):
                s = s_unit(a, h, i)
                if i == 0:
                    pe.wait_ge(stacked[h], 6 * 16 * (a + 1))
                if not fresh or i >= 2:
                    pe.wait_ge(s_max, s - 1)
                mm(psS[i % 2][:, :], Qs[0:KS, h, i * P:(i + 1) * P], Ks[0:KS, h, :],
                   start=True, stop=True).then_inc(s_mm, 1)

            def iteration(g, j, horner, prep, attend, end):
                it = g * IPG + j
                a, p, e = it - ATT, it - PREP, it - END
                for kind, n, i in events(j, horner, prep, attend, end):
                    if kind in ("X1T", "Q", "K", "V"):
                        pe.wait_ge(m_ev, MPB * p + n)
                    if kind == "XT":
                        if n == 0:
                            pe.wait_ge(xin_in, 16 * (g + 1))
                        next_unit(g, U_X + n)
                        for t in range(NT):
                            last = nc.tensor.transpose(psL[n % 2][:, t * P:(t + 1) * P],
                                                       xin[:, n, t, :], ident[:, :])
                        last.then_inc(l0_mm, 1)
                    elif kind == "Z":
                        powers_of_x(g, n)
                    elif kind == "C":
                        next_unit(g, U_C + n)
                        pe.wait_ge(l0_ev[1], EPB * g + U_C // 2)
                        if isinstance(g, int) and g == 0:
                            pe.wait_ge(bias_lo, 2)
                        coefficients(psL[n % 2][:, :], BLK - 1, n, True).then_inc(l0_mm, 1)
                    elif kind == "BC":
                        next_unit(g, U_B + n)
                        coefficients(psL[n % 2][:, :], BLK - 2 - n // UPS, n % UPS, False)
                    elif kind == "BM":
                        join(g, n)
                    elif kind == "X1T":
                        pe.wait_ge(x1_done, p + 1)
                        for t in range(NT):
                            last = nc.tensor.transpose(psM[:, t * P:(t + 1) * P], x1[:, t, :], ident[:, :])
                        last.then_inc(m_mm, 1)
                    elif kind in ("Q", "K"):
                        cols = slice(0, D) if kind == "Q" else slice(D, 2 * D)
                        mm(psM[:, :], W_sb[:, cols], x1T[:, :], start=True, stop=True).then_inc(m_mm, 1)
                    elif kind == "V":
                        cols = slice(2 * D, 3 * D)
                        for t in range(NT):
                            nodes = slice(t * P, (t + 1) * P)
                            last = mm(psM[:, nodes], x1T[:, nodes], W_sb[:, cols], start=True, stop=True)
                        last.then_inc(m_mm, 1)
                    elif kind == "S":
                        scores(a, n, i, False)
                    elif kind == "S0":
                        scores(p, n, i, not attend)
                    elif kind == "TR":
                        r = s_unit(a, n, i)
                        if i == 0:
                            pe.wait_ge(s_exp, s_unit(a, n, NT))
                        if horner or g == NG and j == 0 and n == 0 and i < 2:
                            pe.wait_ge(t_lo, r - 1 + T_FREE)
                        elif g == NG and j == 0 and n == 0:
                            pe.wait_ge(l0_ev[i % 2], EPB * NG)
                        else:
                            pe.wait_ge(t_lo, r - 3 + T_FREE)
                        for t in range(NT):
                            last = nc.tensor.transpose(e_bank(horner, i)[:, t * P:(t + 1) * P],
                                                       E[:, n % 2, t, i * P:(i + 1) * P], ident[:, :])
                        last.then_inc(t_mm, 1)
                    elif kind in ("PV", "PVF"):
                        b, parity = (a, 1 - j) if kind == "PV" else (e, j)
                        pe.wait_ge(t_lo, s_unit(b, n, NT) + T_FREE)
                        if n % 2 == 0:
                            pe.wait_ge(c_ev, b * 2 + n // 2 + C_FREE)
                        if n == 0:
                            pe.wait_ge(m_ev, MPB * (b + 1))
                        for t in range(NT):
                            for part in (ETh, ETl):
                                v_at = slice(2 * HD * (n % 2), 2 * HD * (n % 2) + P)
                                last = mm(psO[:, :], V[:, parity, t, n // 2, v_at],
                                          part[:, n % 2, t, :], start=(n % 2 == 0 and t == 0 and part is ETh),
                                          stop=(n % 2 == 1 and t == NT - 1 and part is ETl))
                        if n % 2 == 1:
                            last.then_inc(o_mm, 1)
                    elif kind in ("CB", "CBF"):
                        pe.wait_ge(o_ev, (a if kind == "CB" else e) * 2 + n + 1)
                        for t in range(NT):
                            last = nc.tensor.transpose(psO[:, t * P:(t + 1) * P],
                                                       oT[:, t * P:(t + 1) * P], ident[:, :])
                        last.then_inc(c_mm, 1)

            run_iterations(pe, iteration)

        @block.vector
        def _(dve):
            V_ = nc.vector

            dve.wait_ge(in_w, 32)
            V_.tensor_scalar(dclip[:, :], dcol[:, :], 0.0, 1.0, ALU.max, ALU.min).then_inc(c_vec, 1)
            dve.wait_ge(c_pe, 1)
            dve.wait_ge(c_vec, 1)
            V_.tensor_copy(wT[:, :], psM[:, 0:D]).then_inc(c_vec, 1)
            V_.tensor_scalar(wdT[:, :], psM[:, 0:D], dclip[:, 0:1], None, ALU.mult).then_inc(c_vec, 1)
            dve.wait_ge(c_ident, 2)
            dve.wait_ge(c_pool, 3)
            for par in range(2):
                V_.tensor_scalar(Rst[:, par, 0, 0:D], ident[:, :], DT, None, ALU.mult)
            V_.tensor_scalar(decay_ident[:, :], ident[:, :], 1.0 - DT, None, ALU.mult).then_inc(c_vec, 1)
            dve.wait_ge(c_vec, 4)
            dve.wait_ge(c_pe, 2)
            V_.scalar_tensor_tensor(out=Qm[:, :], in0=psM[:, 0:D], scalar=DT, in1=decay_ident[:, :],
                                    op0=ALU.mult, op1=ALU.add).then_inc(rec_ev, 1)
            dve.wait_ge(c_act, 1)
            V_.tensor_scalar(nrate[:, :], rate[:, :], -DT / 4, -DT / 4, ALU.mult, ALU.add).then_inc(r_done, 1)
            dve.wait_ge(r_done, 1)
            V_.tensor_scalar(rate[:, :], nrate[:, :], -1.0, None, ALU.mult).then_inc(r_done, 1)

            def recurrence(t):
                old, new = t % 2, (t + 1) % 2
                dve.wait_ge(rec_mm, t + 1)
                dve.wait_ge(rec_ev, t + 1)
                for c in range(t // 3 + 1):
                    k0, k1 = 3 * c, min(3 * c + 3, t + 1)
                    V_.tensor_tensor(Rst[:, new, 1 + k0:1 + k1, :],
                                     R_BANKS[c][:, 0:(k1 - k0) * SLOT].rearrange("p (k s) -> p k s", s=SLOT),
                                     Rst[:, old, k0:k1, :], ALU.add)
                V_.tensor_copy(Rst[:, new, 2 + t, :], Rst[:, old, 1 + t, :]).then_inc(rec_ev, 1)

            def power_low(i, m):
                dve.wait_ge(pt_hi, i * NT + m + 1)
                V_.tensor_tensor(PTl[:, i, m, :], P_BANKS[m][:, :], f(PTh[:, i, m, :]),
                                 ALU.subtract).then_inc(pt_lo, 1)

            dve.wait_ge(r_done, 2)
            for t in range(NT):
                dve.wait_ge(in_adj[t], 16)
                V_.tensor_scalar(P_sb[:, t, :], adj_sb[:, t, :], rate[:, t:t + 1], None,
                                 ALU.mult).then_inc(r_done, 1)
                dve.wait_ge(r_done, 3 + t)
                diag = P_sb[:, t, t * P:(t + 1) * P]
                V_.scalar_tensor_tensor(out=diag, in0=ident[:, :], scalar=nrate[:, t:t + 1], in1=diag,
                                        op0=ALU.mult, op1=ALU.add).then_inc(p_sb, 1)
            for m in range(NT):
                power_low(0, m)
            dve.wait_ge(in_fc, 32)
            recurrence(0)
            for m in range(NT):
                power_low(1, m)
                recurrence(1 + m)
            for m in range(NT - 1):
                power_low(2, m)
                recurrence(5 + m)
            power_low(2, NT - 1)
            dve.wait_ge(c_pool, 4)
            dve.wait_ge(rec_ev, STEPS + 1)
            last_r = Rst[:, STEPS % 2]
            for h in range(3):
                k_cols = bass.AP(x1res, bcols.offset + h * QUAD,
                                 [list(bcols.ap[0]), [3 * QUAD + PW, BLK], [1, PW]])
                ins = V_.tensor_copy(k_cols, last_r[:, 1:1 + RS, D].rearrange("p (q i) -> p q i", i=PW))
            ins.then_inc(bias_in, 1)
            V_.tensor_tensor(last_r[:, 1, 0:D], last_r[:, 1, 0:D], ident[:, :], ALU.add).then_inc(bias_in, 1)
            dve.wait_ge(bias_hi, 1)
            V_.tensor_tensor(Wst[QUAD:2 * QUAD, :], psM[QUAD:2 * QUAD, :], f(Wst[QUAD:2 * QUAD, :]),
                             ALU.subtract).then_inc(bias_lo, 1)
            dve.wait_ge(bias_hi, 2)
            V_.tensor_tensor(rb[2 * QUAD:3 * QUAD, :, :], psM[2 * QUAD:3 * QUAD, 0:BLK * D].rearrange(
                "p (q d) -> p q d", d=D), f(rb[2 * QUAD:3 * QUAD, :, :]), ALU.subtract).then_inc(bias_lo, 1)
            dve.wait_ge(c_pool, 10)
            V_.tensor_scalar(mask[:, :, :], adj_sb, 0.0, NEG, ALU.is_equal, ALU.mult).then_inc(c_vec, 1)
            dve.wait_ge(c_vec, 5)
            dve.wait_ge(rt_ev, 3)
            V_.memset(rec[:, :], 0.0).then_inc(t_lo, T_FREE)
            V_.memset(y[:, :, :], 0.0).then_inc(y_out, Y_FREE)
            V_.memset(negmax[:, :], 0.0).then_inc(c_ev, C_FREE)

            def low(bank_ap, hi, dst):
                return V_.tensor_tensor(dst, bank_ap, f(hi), ALU.subtract)

            def moments(which, count, src):
                s = ln[which]
                for t in range(NT):
                    ins = V_.bn_stats(stats[:, which, t, :], src(t))
                ins.then_inc(s, 1)
                dve.wait_ge(s, 3 * count + 1)
                carry_waits(dve, dve_passed)
                for t in range(NT):
                    ins = V_.bn_aggr(mv[:, which, t, :], stats[:, which, t, :])
                ins.then_inc(s, 1)
                dve.wait_ge(s, 3 * count + 2)
                V_.tensor_scalar(var[:, which, :], mv[:, which, :, 1], EPS, None, ALU.add).then_inc(s, 1)

            def normalise(which, count, src, dst):
                dve.wait_ge(root[which], count + 1)
                for t in range(NT):
                    ins = V_.tensor_scalar(dst(t), src(t), mv[:, which, t, 0:1],
                                           rstd[:, which, t:t + 1], ALU.subtract, ALU.mult)
                return ins

            def maximum(a, h, i, fresh):
                s = s_unit(a, h, i)
                at = h * NT + i
                dve.wait_ge(s_mm, s + 1)
                if not fresh or i >= 2:
                    dve.wait_ge(s_exp, s - 1)
                carry_waits(dve, dve_passed)
                V_.tensor_tensor_reduce(out=Sm[:, i % 2, :], in0=psS[i % 2][:, :], in1=mask[:, i, :],
                                        scale=-SCALE, scalar=3e38, op0=ALU.add, op1=ALU.min,
                                        accum_out=negmax[:, at:at + 1]).then_inc(s_max, 1)

            def iteration(g, j, horner, prep, attend, end):
                it = g * IPG + j
                a, p, e = it - ATT, it - PREP, it - END
                for kind, n, i in events(j, horner, prep, attend, end):
                    if kind == "C" or kind == "BM" and n < (BLK - 2) * UPS:
                        number = n if kind == "C" else UPS + n
                        dve.wait_ge(l0_hi, (BLK - 1) * UPS * g + number + 1)
                        low(psL[n % 2][:, :], Yh[:, number // UPS, units(n), :],
                            Yl[:, number // UPS, units(n), :]).then_inc(l0_ev[n % 2], 1)
                    elif kind == "LN1A":
                        for bank_ev in l0_ev:
                            dve.wait_ge(bank_ev, EPB * g)
                        moments(0, p, lambda t: u[:, t, j * D:(j + 1) * D])
                    elif kind == "LN1B":
                        dve.wait_ge(x1_kept, p)
                        normalise(0, p, lambda t: u[:, t, j * D:(j + 1) * D],
                                  lambda t: x1[:, t, :]).then_inc(x1_done, 1)
                    elif kind in ("QL", "KL", "VL"):
                        dve.wait_ge(m_hi, (MPB - 1) * p + n)
                        if kind == "VL":
                            for e_ in range(2):
                                ins = low(v_part(psM, e_), V[:, j, :, :, 4 * HD * e_:4 * HD * e_ + HD],
                                          V[:, j, :, :, 4 * HD * e_ + HD:4 * HD * e_ + 2 * HD])
                            ins.then_inc(m_ev, 1)
                        else:
                            h_, l_ = {"QL": (qh, ql), "KL": (kh, kl)}[kind]
                            low(psM[:, :], h_[:, :], l_[:, :]).then_inc(m_ev, 1)
                    elif kind == "S":
                        maximum(a, n, i, False)
                    elif kind == "S0":
                        maximum(p, n, i, not attend)
                    elif kind == "TR":
                        dve.wait_ge(t_hi, s_unit(a, n, i) + 1)
                        low(e_bank(horner, i)[:, :], ETh[:, n % 2, i, :], ETl[:, n % 2, i, :]).then_inc(t_lo, 1)
                    elif kind in ("CB", "CBF"):
                        b, parity = (a, 1 - j) if kind == "CB" else (e, j)
                        done = b * 2 + n + 1
                        dve.wait_ge(c_mm, done)
                        parts = psO[:, :].rearrange("p (t e l d) -> p t e l d", e=2, l=2, d=HD)
                        V_.tensor_copy(o_sum[:, :, :, :], parts[:, :, :, 0, :]).then_inc(r_done, 1)
                        V_.reciprocal(rec[:, :], sums[:, parity, n * 2 * NT:(n + 1) * 2 * NT]).then_inc(r_done, 1)
                        dve.wait_ge(r_done, 6 + 2 * done)
                        V_.tensor_tensor(o_sum[:, :, :, :], o_sum[:, :, :, :], parts[:, :, :, 1, :],
                                         ALU.add).then_inc(c_ev, 1)
                        dve.wait_ge(c_ev, done + C_FREE)
                        r_b = bass.AP(rec, 0, [list(rec[:, :].ap[0]), [1, NT], [NT, 2], [0, HD]])
                        V_.tensor_tensor(
                            att[:, :, n * 2 * HD:(n + 1) * 2 * HD].rearrange("p t (e d) -> p t e d", e=2),
                            o_sum[:, :, :, :], r_b, ALU.mult).then_inc(att_done, 1)
                    elif kind == "LN2A":
                        dve.wait_ge(x1_kept, e + 1)
                        dve.wait_ge(att_done, e * 2 + 2)
                        V_.tensor_tensor(att[:, :, :], att[:, :, :], x1res[:, j, :, :], ALU.add).then_inc(z_done, 1)
                        dve.wait_ge(z_done, e + 1)
                        moments(1, e, lambda t: att[:, t, :])
                    elif kind == "LN2B":
                        dve.wait_ge(y_out, 16 * e + Y_FREE)
                        normalise(1, e, lambda t: att[:, t, :], lambda t: y[:, t, :]).then_inc(y_done, 1)

            run_iterations(dve, iteration)


_INS = ["x", "adj", "L0_gnn_alpha_train", "L0_gnn_w", "L0_gnn_d", "L0_gnn_fc_in_w", "L0_gnn_fc_in_b", "L1_gnn_W"]


def kernel(**inputs):
    import numpy as _np
    import concourse.bacc as _bacc
    from concourse import mybir as _mybir
    from concourse.bass_utils import run_bass_kernel_spmd as _run

    nc = _bacc.Bacc("TRN2", target_bir_lowering=False, num_devices=1)
    arrays, args = {}, []
    for name in _INS:
        a = _np.ascontiguousarray(inputs[name])
        arrays[f"in_{name}_dram"] = a
        args.append(nc.dram_tensor(f"in_{name}_dram", a.shape, _mybir.dt.from_np(a.dtype), kind="ExternalInput").ap())
    args.append(nc.dram_tensor("out_0_dram", (B, N, D), _mybir.dt.float32, kind="ExternalOutput").ap())
    gnn_kernel(nc, *args)
    r = _run(nc, [arrays], core_ids=[0])
    return r.results[0]["out_0_dram"]
```
